# Optimizing a Trainium2 kernel written in Bass

```python
import numpy as np
import jax
import jax.numpy as jnp

def _softmax(x, axis=-1):
    return jax.nn.softmax(x, axis=axis)

def _gelu(x):
    return jax.nn.gelu(x, approximate=True)

def _silu(x):
    return jax.nn.silu(x)

def _sigmoid(x):
    return jax.nn.sigmoid(x)

def _layernorm(x, axis=-1, eps=1e-05):
    m = jnp.mean(x, axis=axis, keepdims=True)
    v = jnp.var(x, axis=axis, keepdims=True)
    return (x - m) / jnp.sqrt(v + eps)

def _scatter_add(tgt, idx, src, axis=0):
    return tgt.at[idx].add(src)

def _segment_sum(src, seg, n):
    return jax.ops.segment_sum(src, seg, n)
kernel_name = 'mk_early_fusion_d1_tok_img768_r4_9acc3d'

def setup_inputs(seed: int=0):
    np.random.seed(seed)
    _w = jnp.asarray

    def _rec_inputs():
        import jax
        import jax.numpy as jnp
        _rk = jax.random.key(seed)
        x = 1.64766e-05 + 1.00005 * jax.random.normal(jax.random.fold_in(_rk, 1), (8, 3, 512, 192), jnp.float32)
        txt = -0.000331106 + 0.408041 * jax.random.normal(jax.random.fold_in(_rk, 2), (8, 128, 192), jnp.float32)
        return (x, txt)
    x, txt = _rec_inputs()

    def _L0_tok_setup():
        import jax, jax.numpy as jnp
        import numpy as np
        NUM_BANDS = 6
        D_MODEL = 192
        B, N = (2, 512)
        IN_FEATURES = 3 * NUM_BANDS * 2 * D_MODEL
        key = jax.random.key(seed)
        k_xyz, k_w = jax.random.split(key)
        xyz = jax.random.normal(k_xyz, (B, 3, N, D_MODEL), dtype=jnp.float32)
        freq_bands = 2.0 ** jnp.linspace(0.0, NUM_BANDS - 1, NUM_BANDS).astype(jnp.float32)
        bound = 1.0 / np.sqrt(IN_FEATURES)
        W = jax.random.uniform(k_w, (D_MODEL, IN_FEATURES), dtype=jnp.float32, minval=-bound, maxval=bound)
        return {'xyz': xyz, 'freq_bands': freq_bands, 'W': W}
    _L0_tok_all = _L0_tok_setup()
    _L0_tok_in = {k: v for k, v in _L0_tok_all.items() if k in ('freq_bands', 'W')}
    del _L0_tok_all

    def _L0_attn_setup():
        import jax, jax.numpy as jnp
        import numpy as np
        DIM, HEADS, DH, G = (192, 12, 64, 4)
        INNER = HEADS * DH
        B, N = (8, 1024)
        LN_EPS = 1e-05

        def _ln(x, g, b):
            m = x.mean(-1, keepdims=True)
            v = ((x - m) ** 2).mean(-1, keepdims=True)
            return (x - m) * jax.lax.rsqrt(v + LN_EPS) * g + b

        def _phi(x):
            return jnp.concatenate([jax.nn.relu(x), jax.nn.relu(-x)], axis=-1)
        key = jax.random.key(seed)
        ks = jax.random.split(key, 12)
        s = 0.02
        return {'x': jax.random.normal(ks[0], (B, N, DIM), jnp.float32), 'Wk': jax.random.normal(ks[1], (DIM, INNER), jnp.float32) * s, 'Wv': jax.random.normal(ks[2], (DIM, INNER), jnp.float32) * s, 'Wq': jax.random.normal(ks[3], (G, DIM, INNER), jnp.float32) * s, 'Wt': jax.random.normal(ks[4], (G, DH, DH), jnp.float32) * s, 'bt': jax.random.normal(ks[5], (G, DH), jnp.float32) * s, 'gt': jnp.ones((G, DH), jnp.float32), 'betat': jnp.zeros((G, DH), jnp.float32), 'Wf': jax.random.normal(ks[6], (G * INNER, INNER), jnp.float32) * s, 'bf': jax.random.normal(ks[7], (INNER,), jnp.float32) * s, 'gf': jnp.ones((INNER,), jnp.float32), 'betaf': jnp.zeros((INNER,), jnp.float32), 'Wo': jax.random.normal(ks[8], (INNER, DIM), jnp.float32) * s, 'bo': jax.random.normal(ks[9], (DIM,), jnp.float32) * s}
    _L0_attn_all = _L0_attn_setup()
    _L0_attn_in = {k: v for k, v in _L0_attn_all.items() if k in ('Wk', 'Wv', 'Wq', 'Wt', 'bt', 'gt', 'betat', 'Wf', 'bf', 'gf', 'betaf', 'Wo', 'bo')}
    del _L0_attn_all

    def _L0_ffn_setup():
        import jax, jax.numpy as jnp
        import numpy as np
        EPS = 1e-06

        def l2_normalize(x, axis):
            norm = jnp.sqrt(jnp.square(x).sum(axis=axis, keepdims=True))
            return x * (1.0 / (norm + EPS))
        key = jax.random.key(seed)
        ks = jax.random.split(key, 8)
        b, m, d = (32, 256, 192)
        n, p = (8, 4)
        h = d // 8
        X = jax.random.normal(ks[0], (b, m, d), dtype=jnp.float32)
        std_slot = float(np.sqrt(2.0 / (d + n * p)))
        slot_params = jax.random.normal(ks[1], (d, n, p), dtype=jnp.float32) * std_slot
        scale = jnp.ones((), dtype=jnp.float32)
        W_down = jax.random.normal(ks[2], (n, d, h), dtype=jnp.float32) * float(np.sqrt(1.0 / d))
        b_down = jnp.zeros((n, h), dtype=jnp.float32)
        W_up = jax.random.normal(ks[3], (n, h, d), dtype=jnp.float32) * float(np.sqrt(1.0 / h))
        b_up = jnp.zeros((n, d), dtype=jnp.float32)
        return {'X': X, 'slot_params': slot_params, 'scale': scale, 'W_down': W_down, 'b_down': b_down, 'W_up': W_up, 'b_up': b_up}
    _L0_ffn_all = _L0_ffn_setup()
    _L0_ffn_in = {k: v for k, v in _L0_ffn_all.items() if k in ('slot_params', 'scale', 'W_down', 'b_down', 'W_up', 'b_up')}
    del _L0_ffn_all
    return {'x': x, 'txt': txt, 'L0_tok_freq_bands': _L0_tok_in['freq_bands'], 'L0_tok_W': _L0_tok_in['W'], 'L0_attn_Wk': _L0_attn_in['Wk'], 'L0_attn_Wv': _L0_attn_in['Wv'], 'L0_attn_Wq': _L0_attn_in['Wq'], 'L0_attn_Wt': _L0_attn_in['Wt'], 'L0_attn_bt': _L0_attn_in['bt'], 'L0_attn_gt': _L0_attn_in['gt'], 'L0_attn_betat': _L0_attn_in['betat'], 'L0_attn_Wf': _L0_attn_in['Wf'], 'L0_attn_bf': _L0_attn_in['bf'], 'L0_attn_gf': _L0_attn_in['gf'], 'L0_attn_betaf': _L0_attn_in['betaf'], 'L0_attn_Wo': _L0_attn_in['Wo'], 'L0_attn_bo': _L0_attn_in['bo'], 'L0_ffn_slot_params': _L0_ffn_in['slot_params'], 'L0_ffn_scale': _L0_ffn_in['scale'], 'L0_ffn_W_down': _L0_ffn_in['W_down'], 'L0_ffn_b_down': _L0_ffn_in['b_down'], 'L0_ffn_W_up': _L0_ffn_in['W_up'], 'L0_ffn_b_up': _L0_ffn_in['b_up']}

def reference(x, txt, L0_tok_freq_bands, L0_tok_W, L0_attn_Wk, L0_attn_Wv, L0_attn_Wq, L0_attn_Wt, L0_attn_bt, L0_attn_gt, L0_attn_betat, L0_attn_Wf, L0_attn_bf, L0_attn_gf, L0_attn_betaf, L0_attn_Wo, L0_attn_bo, L0_ffn_slot_params, L0_ffn_scale, L0_ffn_W_down, L0_ffn_b_down, L0_ffn_W_up, L0_ffn_b_up):
    import jax
    import jax.numpy as jnp

    def _L0_tok_ref(xyz, freq_bands, W):
        import jax, jax.numpy as jnp
        import numpy as np
        NUM_BANDS = 6
        D_MODEL = 192
        B, N = (2, 512)
        IN_FEATURES = 3 * NUM_BANDS * 2 * D_MODEL
        b, c, n, d = xyz.shape
        xb = 2.0 * jnp.pi * xyz[..., None] * freq_bands
        feat = jnp.concatenate([jnp.sin(xb), jnp.cos(xb)], axis=-1)
        feat = feat.reshape(b, n, -1)
        return jnp.einsum('bnf,of->bno', feat, W)

    def _L0_attn_ref(x, Wk, Wv, Wq, Wt, bt, gt, betat, Wf, bf, gf, betaf, Wo, bo):
        import jax, jax.numpy as jnp
        import numpy as np
        DIM, HEADS, DH, G = (192, 12, 64, 4)
        INNER = HEADS * DH
        B, N = (8, 1024)
        LN_EPS = 1e-05

        def _ln(x, g, b):
            m = x.mean(-1, keepdims=True)
            v = ((x - m) ** 2).mean(-1, keepdims=True)
            return (x - m) * jax.lax.rsqrt(v + LN_EPS) * g + b

        def _phi(x):
            return jnp.concatenate([jax.nn.relu(x), jax.nn.relu(-x)], axis=-1)
        b, n, _ = x.shape
        k = (x @ Wk).reshape(b, n, HEADS, DH).transpose(0, 2, 1, 3)
        v = (x @ Wv).reshape(b, n, HEADS, DH).transpose(0, 2, 1, 3)
        q = jnp.einsum('bnd,gde->gbne', x, Wq).reshape(G, b, n, HEADS, DH)
        q = q.transpose(0, 1, 3, 2, 4)
        q = jnp.einsum('gbhnd,gde->gbhne', q, Wt) + bt[:, None, None, None, :]
        q = jax.nn.gelu(q, approximate=False)
        q = _ln(q, gt[:, None, None, None, :], betat[:, None, None, None, :])
        qf = _phi(q) / jnp.sqrt(jnp.float32(2 * DH))
        kf = _phi(k)
        kv = jnp.einsum('bhnd,bhnm->bhdm', kf, v)
        out = jnp.einsum('gbhnd,bhdm->gbhnm', qf, kv)
        ksum = kf.sum(axis=2)
        norm = jnp.einsum('gbhnd,bhd->gbhn', qf, ksum)
        out = out / (norm[..., None] + 1e-06)
        out = out.transpose(1, 3, 0, 2, 4).reshape(b, n, G * INNER)
        fused = jax.nn.gelu(_ln(out @ Wf + bf, gf, betaf), approximate=False)
        return fused @ Wo + bo

    def _L0_ffn_ref(X, slot_params, scale, W_down, b_down, W_up, b_up):
        import jax, jax.numpy as jnp
        import numpy as np
        EPS = 1e-06

        def l2_normalize(x, axis):
            norm = jnp.sqrt(jnp.square(x).sum(axis=axis, keepdims=True))
            return x * (1.0 / (norm + EPS))
        b, m, d = X.shape
        _, n, p = slot_params.shape
        Xn = l2_normalize(X, axis=-1)
        sp = l2_normalize(slot_params, axis=1) * scale
        logits = jnp.einsum('bmd,dnp->bmnp', Xn, sp)
        D = jax.nn.softmax(logits, axis=1)
        C = jax.nn.softmax(logits.reshape(b, m, n * p), axis=2).reshape(b, m, n, p)
        X_tilde = jnp.einsum('bmd,bmnp->bnpd', Xn, D)
        H = jax.nn.gelu(jnp.einsum('bnpd,ndh->bnph', X_tilde, W_down) + b_down[None, :, None, :], approximate=False)
        Y_tilde = jnp.einsum('bnph,nhd->bnpd', H, W_up) + b_up[None, :, None, :]
        Y = jnp.einsum('bnpd,bmnp->bmd', Y_tilde, C)
        return Y
    h = _L0_tok_ref(x, L0_tok_freq_bands, L0_tok_W)
    h = jnp.concatenate([h, txt], axis=1)
    h = h + _L0_attn_ref(_layernorm(h, axis=-1), L0_attn_Wk, L0_attn_Wv, L0_attn_Wq, L0_attn_Wt, L0_attn_bt, L0_attn_gt, L0_attn_betat, L0_attn_Wf, L0_attn_bf, L0_attn_gf, L0_attn_betaf, L0_attn_Wo, L0_attn_bo)
    h = h + _L0_ffn_ref(_layernorm(h, axis=-1), L0_ffn_slot_params, L0_ffn_scale, L0_ffn_W_down, L0_ffn_b_down, L0_ffn_W_up, L0_ffn_b_up)
    return h

_drawn_inputs = setup_inputs


def setup_inputs(seed=0):
    import zlib

    import numpy as np

    out = dict(_drawn_inputs(seed))
    spreads = {'L0_attn_gt': (1.0, 0.553),
     'L0_attn_betat': (0.0, 0.492),
     'L0_attn_gf': (1.0, 0.2),
     'L0_attn_betaf': (0.0, 0.1),
     'L0_ffn_b_down': (0.0, 0.1),
     'L0_ffn_b_up': (0.0, 0.1)}
    factors = {'L0_ffn_slot_params': 4.677, 'L0_ffn_W_down': 3.955}
    for name, (base, spread) in spreads.items():
        noise = np.random.default_rng([zlib.crc32(name.encode()), seed]).standard_normal(out[name].shape)
        drawn = base * np.exp(spread * noise) if base else spread * noise
        out[name] = jnp.asarray(drawn.astype(out[name].dtype))
    for name, factor in factors.items():
        out[name] = (out[name] * factor).astype(out[name].dtype)
    return out
```

```python
from contextlib import ExitStack

import concourse.bass as bass
from concourse import mybir

F32 = mybir.dt.float32
I32 = mybir.dt.int32
BF16 = mybir.dt.bfloat16
ALU = mybir.AluOpType
ACT = mybir.ActivationFunctionType
AX_X = mybir.AxisListType.X

P = 128
BATCH, NIMG, NTXT, DIM = 8, 512, 128, 192
NTOK = NIMG + NTXT
TPB = NTOK // P
TILES = BATCH * TPB
TAIL = DIM - P

BANDS = 6
COORDS = 3 * DIM
FEATS = COORDS * 2 * BANDS
FULL = COORDS // P
SLOTS = 2 * FULL + 1
HALF = 256
ROUND = 1.5 * 2.0 ** 23
SIGN_BIT = -2 ** 31
TWO_PI = 6.283185307179586

HEADS, DH, G = 12, 64, 4
INNER = HEADS * DH
GH = G * HEADS
QCOLS = G * INNER
KVW = DH + 1
LN_EPS = 1e-5
NORM_EPS = 1e-6 * (2 * DH) ** 0.5

EXPERTS, SLOTP, HID = 8, 4, DIM // 8
NP_ = EXPERTS * SLOTP
L2_EPS = 1e-6


def tokenizer(nc, x, txt, bands, tok_w, h, ident):
    with ExitStack() as ctx:
        def sb(name, shape, dt):
            return ctx.enter_context(nc.sbuf_tensor(name, shape, dt))

        def sem(name):
            return ctx.enter_context(nc.semaphore(name))

        w_hi = sb("w_hi", [P, BANDS, SLOTS, DIM], BF16)
        w_lo = sb("w_lo", [P, BANDS, SLOTS, DIM], BF16)
        w_f = sb("w_f", [P, BANDS, SLOTS, DIM], F32)
        fr = sb("fr", [P, BANDS], F32)
        NCH = FULL + 1
        RING = 3
        xt = sb("xt", [P, 2, NCH, HALF], F32)
        quarter = sb("quarter", [P, 1], F32)
        near = sb("near", [P, NCH, HALF], F32)
        turns = sb("turns", [P, 2, SLOTS, HALF], F32)
        feat = sb("feat", [P, RING, SLOTS, HALF], F32)
        f_hi = sb("f_hi", [P, RING, SLOTS, HALF], BF16)
        f_lo = sb("f_lo", [P, RING, SLOTS, HALF], BF16)
        acc = ctx.enter_context(nc.psum_tensor("acc", [P, 2, 2, 512], F32))
        x_in = [sem(f"x_in{i}") for i in range(2)]
        w_in = [sem(f"w_in{i}") for i in range(BANDS)]
        bands_in, txt_in = sem("bands_in"), sem("txt_in")
        zeroed, ident_ready = sem("zeroed"), sem("ident_ready")
        w_hi_ready, w_lo_ready = sem("w_hi_ready"), sem("w_lo_ready")
        shifted = sem("shifted")
        rounded = sem("rounded")
        reduced = sem("reduced")
        cos_ready = sem("cos_ready")
        hi_ready = sem("f_hi_ready")
        sin_ready = sem("sin_ready")
        quarter_ready = sem("quarter_ready")
        lo_ready = sem("lo_ready")
        multiplied = sem("multiplied")
        h_ready = sem("h_ready")
        STEPS = 2 * BANDS

        with nc.Block() as block:
            @block.sync
            def _(sp):
                def load(b, u):
                    sp.dma_start(xt[:, u], x[b, u]).then_inc(x_in[u], 16)

                sp.dma_start(fr[:, :], bands.partition_broadcast(P)).then_inc(bands_in, 16)
                load(0, 0)
                for i in range(BANDS):
                    sp.dma_start(w_f[:, i], tok_w[:, i]).then_inc(w_in[i], 16)
                    if i == 0:
                        load(0, 1)
                for b in range(BATCH):
                    sp.dma_start(h[:, TPB * b + TPB - 1, :], txt[b]).then_inc(txt_in, 16)
                with sp.Fori(1, BATCH) as b:
                    for u in range(2):
                        sp.wait_ge(reduced, BANDS * (2 * b + u - 1))
                        load(b, u)
                sp.wait_ge(txt_in, 16 * BATCH)

            @block.tensor
            def _(pe):
                def batch(b):
                    for u in range(2):
                        for i in range(BANDS):
                            s = STEPS * b + BANDS * u + i
                            pe.wait_ge(hi_ready, s + 1)
                            if isinstance(b, int) and u == 0:
                                pe.wait_ge(w_lo_ready, i + 1)
                            if i == 0 and not (isinstance(b, int) and b == 0):
                                pe.wait_ge(h_ready, 2 * b + u - 1)
                            for t in range(2):
                                for k in range(SLOTS):
                                    hi = f_hi[:, i % RING, k, t * P:(t + 1) * P]
                                    nc.tensor.matmul(acc[:, u, t, 0:DIM], hi, w_hi[:, i, k, :],
                                                     start=i == 0 and k == 0, stop=False)
                                    nc.tensor.matmul(acc[:, u, t, 0:DIM], hi, w_lo[:, i, k, :], start=False, stop=False)
                            pe.wait_ge(lo_ready, s + 1)
                            for t in range(2):
                                for k in range(SLOTS):
                                    lo = f_lo[:, i % RING, k, t * P:(t + 1) * P]
                                    last = nc.tensor.matmul(acc[:, u, t, 0:DIM], lo, w_hi[:, i, k, :], start=False,
                                                            stop=i == BANDS - 1 and k == SLOTS - 1)
                            last.then_inc(multiplied, 1)

                batch(0)
                with pe.Fori(1, BATCH) as b:
                    batch(b)

            @block.scalar
            def _(act):
                def store_h(b, u):
                    act.wait_ge(multiplied, STEPS * b + BANDS * (u + 1))
                    nc.scalar.activation(h[:, bass.ds(TPB * b + 2 * u, 2), :], acc[:, u, :, 0:DIM],
                                         ACT.Copy).then_inc(h_ready, 1)

                def batch(b, first_batch):
                    for u in range(2):
                        for i in range(BANDS):
                            if first_batch and u == 0:
                                act.wait_ge(w_in[i], 16)
                                nc.scalar.activation(w_hi[:, i], w_f[:, i], ACT.Copy).then_inc(w_hi_ready, 1)
                            s = STEPS * b + BANDS * u + i
                            early = first_batch and u == 0 and i < RING
                            act.wait_ge(cos_ready, s + 1)
                            if not early:
                                act.wait_ge(multiplied, s + 1 - RING)
                            nc.scalar.activation(f_hi[:, i % RING, 0:FULL], turns[:, i % 2, 0:FULL], ACT.Sin,
                                                 scale=TWO_PI)
                            nc.scalar.activation(f_hi[:, i % RING, FULL:SLOTS], turns[:, i % 2, FULL:SLOTS], ACT.Sin,
                                                 bias=quarter[:, 0:1], scale=TWO_PI).then_inc(hi_ready, 1)
                            if not early:
                                act.wait_ge(lo_ready, s + 1 - RING)
                            nc.scalar.activation(feat[:, i % RING, 0:FULL], turns[:, i % 2, 0:FULL], ACT.Sin,
                                                 scale=TWO_PI)
                            nc.scalar.activation(feat[:, i % RING, FULL:SLOTS], turns[:, i % 2, FULL:SLOTS], ACT.Sin,
                                                 bias=quarter[:, 0:1], scale=TWO_PI).then_inc(sin_ready, 1)
                            if i == 2 and not (first_batch and u == 0):
                                store_h(b + u - 1, 1 - u)

                act.wait_ge(quarter_ready, 1)
                batch(0, True)
                with act.Fori(1, BATCH) as b:
                    batch(b, False)
                store_h(BATCH - 1, 1)

            @block.vector
            def _(dve):
                def reduce(b, u, i, first):
                    s = STEPS * b + BANDS * u + i
                    f = fr[:, i:i + 1]
                    if i == 0:
                        dve.wait_ge(x_in[u], 16 * b + 16)
                    if not (first and s == 0):
                        dve.wait_ge(reduced, s)
                    nc.vector.tensor_scalar(near[:, :, :], xt[:, u], f, ROUND, ALU.mult, ALU.add).then_inc(shifted, 1)
                    dve.wait_ge(shifted, s + 1)
                    nc.vector.tensor_scalar(near[:, :, :], near[:, :, :], ROUND, None, ALU.subtract).then_inc(rounded, 1)
                    dve.wait_ge(rounded, s + 1)
                    if not (first and s < 2):
                        dve.wait_ge(sin_ready, s - 1)
                    nc.vector.scalar_tensor_tensor(
                        out=turns[:, i % 2, 0:NCH, :].rearrange("p c n -> p (c n)"),
                        in0=xt[:, u].rearrange("p c n -> p (c n)"), scalar=f,
                        in1=near[:, :, :].rearrange("p c n -> p (c n)"),
                        op0=ALU.mult, op1=ALU.subtract).then_inc(reduced, 1)
                    dve.wait_ge(reduced, s + 1)
                    bits = turns[:, i % 2].bitcast(I32)
                    nc.vector.tensor_scalar(bits[:, NCH:SLOTS, :], bits[:, 0:FULL, :], SIGN_BIT, None, ALU.bitwise_or)
                    nc.vector.tensor_scalar(bits[P - TAIL:P, FULL, :], bits[P - TAIL:P, FULL, :], SIGN_BIT, None,
                                            ALU.bitwise_or)
                    nc.vector.tensor_scalar(turns[0:P - TAIL, i % 2, FULL, :], turns[0:P - TAIL, i % 2, FULL, :],
                                            0.25, None, ALU.subtract).then_inc(cos_ready, 1)

                def batch(b, first, last_batch):
                    for u in range(2):
                        for i in range(BANDS):
                            if i < BANDS - 1:
                                reduce(b, u, i + 1, first)
                            elif u == 0:
                                reduce(b, 1, 0, first)
                            elif not last_batch:
                                reduce(b + 1, 0, 0, False)

                dve.wait_ge(bands_in, 16)
                nc.vector.memset(quarter[:, :], TWO_PI / 4).then_inc(quarter_ready, 1)
                reduce(0, 0, 0, True)
                batch(0, True, False)
                with dve.Fori(1, BATCH - 1) as b:
                    batch(b, False, False)
                batch(BATCH - 1, False, True)

            @block.gpsimd
            def _(pool):
                nc.gpsimd.memset(ident[:, :], 0.0).then_inc(zeroed, 1)
                pool.wait_ge(zeroed, 1)
                nc.gpsimd.affine_select(out=ident[:, :], in_=ident[:, :], compare_op=ALU.not_equal, fill=1.0,
                                        base=0, pattern=[[-1, P]], channel_multiplier=1).then_inc(ident_ready, 1)

                def batch(b, first):
                    for u in range(2):
                        for i in range(BANDS):
                            if first and u == 0:
                                pool.wait_ge(w_hi_ready, i + 1)
                                nc.gpsimd.tensor_tensor(w_lo[:, i], w_f[:, i], w_hi[:, i],
                                                        ALU.subtract).then_inc(w_lo_ready, 1)
                            s = STEPS * b + BANDS * u + i
                            pool.wait_ge(sin_ready, s + 1)
                            pool.wait_ge(hi_ready, s + 1)
                            if not (first and s < RING):
                                pool.wait_ge(multiplied, s + 1 - RING)
                            nc.gpsimd.tensor_tensor(f_lo[:, i % RING], feat[:, i % RING], f_hi[:, i % RING],
                                                    ALU.subtract).then_inc(lo_ready, 1)

                batch(0, True)
                with pool.Fori(1, BATCH) as b:
                    batch(b, False)


def attention_weights(nc, a, w, stats, h, ident):
    with ExitStack() as ctx:
        def sb(name, shape, dt):
            return ctx.enter_context(nc.sbuf_tensor(name, shape, dt))

        def sem(name):
            return ctx.enter_context(nc.semaphore(name))

        kv_f = sb("kv_f", [P, 2, 2 * INNER], F32)
        wq_t = sb("wq_t", [P, G * HEADS // 2, 2 * P], F32)
        wt = sb("wt_diag", [P, G, P], F32)
        bn = sb("bn", [P, 2, 6], F32)
        bias = wq_t[:, 0:QCOLS // (2 * P), :].rearrange("p n c -> p (n c)")
        wo_f = wq_t[:, QCOLS // (2 * P):, :].rearrange("p n c -> p (n c)")[:, 0:INNER // P * DIM].rearrange(
            "p (c d) -> p c d", d=DIM)
        ps_f = ctx.enter_context(nc.psum_tensor("ps_f", [P, 4, 512], F32))
        kv_in, wq_in, wt_in, bias_in, wo_in, small_in = (sem(n) for n in (
            "kv_in", "wq_in", "wt_in", "bias_in", "wo_in", "small_in"))
        halved, folded, fold_hi, fold_lo = sem("halved"), sem("folded"), sem("fold_hi"), sem("fold_lo")
        kv_hi_done, kv_lo_done, wo_hi_done, wo_lo_done = (sem(n) for n in (
            "kv_hi_done", "kv_lo_done", "wo_hi_done", "wo_lo_done"))
        bias_hi, bias_lo, signs_done = sem("bias_hi"), sem("bias_lo"), sem("signs_done")
        bn_done, mean_done, var_done, rstd_done = sem("bn_done"), sem("mean_done"), sem("var_done"), sem("rstd_done")
        eps_set = sem("eps_set")
        LOW = 96
        PAIRS = G * HEADS // 2

        with nc.Block() as block:
            @block.sync
            def _(sp):
                sp.dma_start(wt[:, :, :], a['wt_diag']).then_inc(wt_in, 16)
                sp.dma_start(wq_t[:, :, :], a['wq_t']).then_inc(wq_in, 16)
                sp.dma_start(kv_f[:, :, :], a['kv_w']).then_inc(kv_in, 16)
                sp.wait_ge(folded, PAIRS)
                sp.dma_start(bias[TAIL:P, :], a['bias_rows']).then_inc(bias_in, 16)
                sp.dma_start(wo_f, a['wo']).then_inc(wo_in, 16)

            @block.scalar
            def _(act):
                for n in ('gt', 'betat', 'gf', 'betaf'):
                    act.dma_start(w[n][:, :], a[n]).then_inc(small_in, 16)
                act.dma_start(w['bf'][:, :], a['bf'].partition_broadcast(P)).then_inc(small_in, 16)
                act.dma_start(w['bo'][:, :], a['bo'].partition_broadcast(P)).then_inc(small_in, 16)
                for u in range(PAIRS):
                    act.wait_ge(folded, u + 1)
                    nc.scalar.activation(w['q_hi'][:, :, u * P:(u + 1) * P],
                                         ps_f[:, u % 4, 0:2 * P].rearrange("p (n c) -> p n c", n=2),
                                         ACT.Copy).then_inc(fold_hi, 1)
                    if u == 3:
                        act.wait_ge(kv_in, 16)
                        nc.scalar.activation(w['kv_hi'], kv_f[:, :, :], ACT.Copy).then_inc(kv_hi_done, 1)
                act.wait_ge(bias_in, 16)
                nc.scalar.activation(w['q_lo'][TAIL:P, 1, :], bias[TAIL:P, :], ACT.Copy).then_inc(bias_hi, 1)
                act.wait_ge(wo_in, 16)
                nc.scalar.activation(w['wo_hi'][:, :, :], wo_f, ACT.Copy).then_inc(wo_hi_done, 1)
                act.wait_ge(small_in, 16 * 6)

            @block.gpsimd
            def _(pool):
                nc.gpsimd.memset(w['half'][:, :], -0.5).then_inc(halved, 1)
                nc.gpsimd.memset(w['eps'][:, :], LN_EPS).then_inc(eps_set, 1)
                pool.wait_ge(kv_hi_done, 1)
                nc.gpsimd.tensor_tensor(w['kv_lo'], kv_f[:, :, :], w['kv_hi'], ALU.subtract).then_inc(kv_lo_done, 1)
                pool.wait_ge(mean_done, TILES)
                nc.gpsimd.tensor_scalar(stats[:, :, 1], stats[:, :, 1], 1.0, LN_EPS, ALU.mult, ALU.add).then_inc(var_done, 1)
                pool.wait_ge(var_done, 1)
                pool.wait_ge(halved, 1)
                nc.gpsimd.tensor_tensor(stats[:, :, 1], stats[:, :, 1], w['half'][:, 0:TILES], ALU.pow).then_inc(rstd_done, 1)
                pool.wait_ge(rstd_done, 1)

            @block.tensor
            def _(pe):
                pe.wait_ge(wt_in, 16)
                pe.wait_ge(wq_in, 16)
                for u in range(PAIRS):
                    if u >= 4:
                        pe.wait_ge(fold_lo, u - 3)
                    for k in range(2):
                        last = nc.tensor.matmul(ps_f[:, u % 4, k * P:(k + 1) * P], wq_t[:, u, k * P:(k + 1) * P],
                                                wt[:, u // (HEADS // 2), :], start=True, stop=True)
                    last.then_inc(folded, 1)

            @block.vector
            def _(dve):
                def row_stats(n):
                    if n >= 2:
                        dve.wait_ge(mean_done, n - 1)
                    nc.vector.bn_stats(bn[:, n % 2, :], h[:, n, :]).then_inc(bn_done, 1)
                    dve.wait_ge(bn_done, n + 1)
                    nc.vector.bn_aggr(stats[:, n, :], bn[:, n % 2, :]).then_inc(mean_done, 1)

                for u in range(PAIRS):
                    dve.wait_ge(fold_hi, u + 1)
                    cols = slice(u * P, (u + 1) * P)
                    src = ps_f[:, u % 4, 0:2 * P].rearrange("p (n c) -> p n c", n=2)
                    nc.vector.tensor_tensor(w['q_lo'][:, 0, cols], src[:, 0], w['q_hi'][:, 0, cols], ALU.subtract)
                    nc.vector.tensor_tensor(w['q_lo'][0:TAIL, 1, cols], src[0:TAIL, 1], w['q_hi'][0:TAIL, 1, cols],
                                            ALU.subtract).then_inc(fold_lo, 1)
                    for n in range(2 * u, min(2 * u + 2, TILES)):
                        row_stats(n)
                dve.wait_ge(bias_hi, 1)
                nc.vector.tensor_tensor(w['q_lo'][LOW:LOW + 1, 1, :], bias[LOW:LOW + 1, :],
                                        w['q_lo'][LOW:LOW + 1, 1, :], ALU.subtract).then_inc(bias_lo, 1)
                dve.wait_ge(wo_hi_done, 1)
                nc.vector.tensor_tensor(w['wo_lo'][:, :, :], wo_f, w['wo_hi'][:, :, :], ALU.subtract).then_inc(wo_lo_done, 1)
                dve.wait_ge(small_in, 16 * 6)
                for n in ('gt', 'betat'):
                    nc.vector.tensor_scalar(w[n][DH:P, :], w[n][DH:P, :], -1.0, None, ALU.mult).then_inc(signs_done, 1)


def keys_and_values(nc, a, w, kv_hi, kv_lo, stats, h, ident):
    HH = HEADS // 2
    HC = HH * DH
    WF_CHUNKS = QCOLS // P
    PER_BATCH = WF_CHUNKS // BATCH
    XBUF = (0, 1, 2, 0, 1)
    KBUF = (0, 1, 2, 0, 1, 2, 0, 1, 2, 3)
    with ExitStack() as ctx:
        def sb(name, shape, dt):
            return ctx.enter_context(nc.sbuf_tensor(name, shape, dt))

        def sem(name):
            return ctx.enter_context(nc.semaphore(name))

        xn = sb("xn", [P, 2 * P], F32)
        xh = sb("xh", [P, 3, 2, P], BF16)
        xl = sb("xl", [P, 3, P], BF16)
        kf = sb("kf", [P, 2, HH, 2, DH], F32)
        kf_hi = sb("kf_hi", [P, 4, HH, 2, DH], BF16)
        kf_lo = sb("kf_lo", [P, 4, HH, 2, DH], BF16)
        v_hi = sb("v_hi", [P, 4, HH, KVW], BF16)
        v_lo = sb("v_lo", [P, 4, HH, KVW], BF16)
        wf_f = sb("wf_f", [P, 2, INNER], F32)
        ps_x = ctx.enter_context(nc.psum_tensor("ps_x2", [P, 512], F32))
        ps_p = ctx.enter_context(nc.psum_tensor("ps_p", [P, 2, 2, 512], F32))
        ps_kv = ctx.enter_context(nc.psum_tensor("ps_kv", [P, 2, 512], F32))
        ones_set, x_norm, x_turned, xh_ready, xl_ready = (sem(n) for n in ("ones_set", "x_norm", "x_turned2", "xh_ready", "xl_ready"))
        projected, kf_ready, kf_hi_ready, kpos_lo_ready, kneg_lo_ready, v_hi_ready, v_lo_ready = (sem(n) for n in (
            "projected", "kf_ready", "kf_hi_ready", "kpos_lo_ready", "kneg_lo_ready", "v_hi_ready", "v_lo_ready"))
        summed, kv_hi_ready, kv_lo_ready = sem("summed"), sem("kv_hi_ready"), sem("kv_lo_ready")
        wf_in = [sem(f"wf_in{i}") for i in range(2)]
        wf_hi_ready, wf_lo_ready = sem("wf_hi_ready"), sem("wf_lo_ready")
        wf = a['wf']
        is0 = lambda v: isinstance(v, int) and v == 0

        with nc.Block() as block:
            @block.sync
            def _(sp):
                def load(b):
                    for k in range(PER_BATCH):
                        before = {0: 0, 1: -1, 2: 1}[k]
                        if not is0(b) or k == 2:
                            sp.wait_ge(wf_lo_ready, PER_BATCH * b + before)
                        sp.dma_start(wf_f[:, k % 2, :], wf[PER_BATCH * b + k]).then_inc(wf_in[k % 2], 16)
                load(0)
                with sp.Fori(1, BATCH) as b:
                    load(b)

            @block.tensor
            def _(pe):
                def turn_x(n):
                    pe.wait_ge(x_norm, n + 1)
                    if not is0(n):
                        pe.wait_ge(xh_ready, n)
                        pe.wait_ge(xl_ready, n)
                    for k in range(2):
                        last = nc.tensor.transpose(ps_x[:, k * P:(k + 1) * P], xn[:, k * P:(k + 1) * P], ident[:, :])
                    last.then_inc(x_turned, 1)

                def project(n, t, hf, early):
                    if hf == 0:
                        pe.wait_ge(xh_ready, n + 1)
                        pe.wait_ge(xl_ready, n + 1)
                    if not early:
                        pe.wait_ge(kf_ready, 2 * n + hf - 1)
                        pe.wait_ge(v_lo_ready, 2 * n + hf - 1)
                    x = XBUF[t]
                    for kv in range(2):
                        cols = slice(kv * INNER + hf * HC, kv * INNER + (hf + 1) * HC)
                        out = ps_p[:, hf, kv, 0:HC]
                        nc.tensor.matmul(out, xh[:, x, 0], w['kv_hi'][:, 0, cols], start=True, stop=False)
                        nc.tensor.matmul(out, xh[:, x, 0], w['kv_lo'][:, 0, cols], start=False, stop=False)
                        nc.tensor.matmul(out, xl[:, x], w['kv_hi'][:, 0, cols], start=False, stop=False)
                        nc.tensor.matmul(out, xh[:, x, 1], w['kv_hi'][:, 1, cols], start=False, stop=False)
                        last = nc.tensor.matmul(out, xh[0:TAIL, x, 1], w['kv_lo'][0:TAIL, 1, cols], start=False, stop=True)
                    last.then_inc(projected, 1)

                def accumulate(b, t, hf, first_batch):
                    for s in (kf_hi_ready, kpos_lo_ready, kneg_lo_ready, v_hi_ready, v_lo_ready):
                        pe.wait_ge(s, 2 * (TPB * b + t) + hf + 1)
                    if t == 0 and not first_batch:
                        pe.wait_ge(kv_lo_ready, 2 * b - 1 + hf)
                    m = KBUF[2 * t + hf]
                    for j in range(HH):
                        out = ps_kv[:, hf, j * KVW:(j + 1) * KVW]
                        ph = kf_hi[:, m, j].rearrange("p s d -> p (s d)")
                        pl = kf_lo[:, m, j].rearrange("p s d -> p (s d)")
                        nc.tensor.matmul(out, ph, v_hi[:, m, j, :], start=t == 0 and j == 0, stop=False,
                                         skip_group_check=True)
                        nc.tensor.matmul(out, ph, v_lo[:, m, j, :], start=False, stop=False, skip_group_check=True)
                        last = nc.tensor.matmul(out, pl, v_hi[:, m, j, :], start=False,
                                                stop=t == TPB - 1 and j == HH - 1, skip_group_check=True)
                    last.then_inc(summed, 1)

                def tile(b, t, first_batch, last_batch):
                    n = TPB * b + t
                    for hf in range(2):
                        project(n, t, hf, first_batch and t == 0)
                        if hf == 0 and not (last_batch and t == TPB - 1):
                            turn_x(n + 1)
                        if t >= 1:
                            accumulate(b, t - 1, hf, first_batch)
                        elif not first_batch:
                            accumulate(b - 1, TPB - 1, hf, False)

                turn_x(0)
                for t in range(TPB):
                    tile(0, t, True, False)
                with pe.Fori(1, BATCH - 1) as b:
                    for t in range(TPB):
                        tile(b, t, False, False)
                for t in range(TPB):
                    tile(BATCH - 1, t, False, True)
                for hf in range(2):
                    accumulate(BATCH - 1, TPB - 1, hf, False)

            @block.scalar
            def _(act):
                def move_x(n, t, early):
                    act.wait_ge(x_turned, n + 1)
                    if not early:
                        act.wait_ge(projected, 2 * n - 2)
                        act.wait_ge(xl_ready, n - 1)
                    nc.scalar.activation(xh[:, XBUF[t]], ps_x[:, 0:2 * P].rearrange("p (k n) -> p k n", k=2),
                                         ACT.Copy).then_inc(xh_ready, 1)

                def key_features(n, t, hf, early):
                    m = KBUF[2 * t + hf]
                    act.wait_ge(projected, 2 * n + hf + 1)
                    if not (early and t == 0):
                        act.wait_ge(kf_hi_ready, 2 * n + hf - 1)
                        act.wait_ge(kpos_lo_ready, 2 * n + hf - 1)
                        act.wait_ge(kneg_lo_ready, 2 * n + hf - 1)
                    src = ps_p[:, hf, 0, 0:HC].rearrange("p (h d) -> p h d", h=HH)
                    nc.scalar.activation(kf[:, hf, :, 0, :], src, ACT.Relu)
                    nc.scalar.activation(kf[:, hf, :, 1, :], src, ACT.Relu, scale=-1.0).then_inc(kf_ready, 1)
                    if not (early and 2 * t + hf < 3):
                        act.wait_ge(summed, 2 * n + hf - 2)
                    nc.scalar.activation(v_hi[:, m, :, 0:DH], ps_p[:, hf, 1, 0:HC].rearrange("p (h d) -> p h d", h=HH),
                                         ACT.Copy).then_inc(v_hi_ready, 1)

                def store_kv(b, hf):
                    act.wait_ge(summed, 2 * TPB * b + 2 * (TPB - 1) + hf + 1)
                    nc.scalar.activation(kv_hi[:, b, hf * HH:(hf + 1) * HH, :],
                                         ps_kv[:, hf, 0:HH * KVW].rearrange("p (h d) -> p h d", h=HH),
                                         ACT.Copy).then_inc(kv_hi_ready, 1)

                def batch(b, first, last):
                    for t in range(TPB):
                        n = TPB * b + t
                        key_features(n, t, 0, first)
                        if t == 1 and not first:
                            store_kv(b - 1, 1)
                        if not (last and t == TPB - 1):
                            move_x(n + 1, (t + 1) % TPB, first and t == 0)
                        key_features(n, t, 1, first)
                        if t == 0 and not first:
                            store_kv(b - 1, 0)
                        if t < PER_BATCH:
                            act.wait_ge(wf_in[t % 2], 16 * b + 16 if t == 1 else 32 * b + 8 * t + 16)
                            nc.scalar.activation(w['wf_hi'][:, PER_BATCH * b + t, :], wf_f[:, t % 2, :],
                                                 ACT.Copy).then_inc(wf_hi_ready, 1)

                act.wait_ge(ones_set, 8)
                move_x(0, 0, True)
                batch(0, True, False)
                with act.Fori(1, BATCH - 1) as b:
                    batch(b, False, False)
                batch(BATCH - 1, False, True)
                store_kv(BATCH - 1, 0)
                store_kv(BATCH - 1, 1)

            @block.vector
            def _(dve):
                def normalize(n):
                    if not is0(n):
                        dve.wait_ge(x_turned, n)
                    nc.vector.tensor_scalar(xn[:, 0:DIM], h[:, n, :], stats[:, n, 0:1], stats[:, n, 1:2],
                                            ALU.subtract, ALU.mult)
                    nc.vector.tensor_scalar(xn[:, DIM:2 * P], h[:, n, P:DIM], stats[:, n, 0:1], stats[:, n, 1:2],
                                            ALU.subtract, ALU.mult).then_inc(x_norm, 1)

                def low_x(n, t):
                    x = XBUF[t]
                    dve.wait_ge(xh_ready, n + 1)
                    nc.vector.tensor_tensor(xl[:, x], ps_x[:, 0:P], xh[:, x, 0, :], ALU.subtract)
                    nc.vector.tensor_tensor(xh[TAIL:P, x, 1, :], ps_x[TAIL:P, P:2 * P], xh[TAIL:P, x, 1, :],
                                            ALU.subtract).then_inc(xl_ready, 1)

                def halves(n, t, hf, early):
                    m = KBUF[2 * t + hf]
                    dve.wait_ge(kf_ready, 2 * n + hf + 1)
                    if not (early and 2 * t + hf < 3):
                        dve.wait_ge(summed, 2 * n + hf - 2)
                    nc.vector.tensor_copy(kf_hi[:, m], kf[:, hf]).then_inc(kf_hi_ready, 1)
                    dve.wait_ge(kf_hi_ready, 2 * n + hf + 1)
                    nc.vector.tensor_tensor(kf_lo[:, m, :, 1, :], kf[:, hf, :, 1, :], kf_hi[:, m, :, 1, :],
                                            ALU.subtract).then_inc(kneg_lo_ready, 1)
                    dve.wait_ge(v_hi_ready, 2 * n + hf + 1)
                    nc.vector.tensor_tensor(v_lo[:, m, :, 0:DH], ps_p[:, hf, 1, 0:HC].rearrange("p (h d) -> p h d", h=HH),
                                            v_hi[:, m, :, 0:DH], ALU.subtract).then_inc(v_lo_ready, 1)

                def store_kv(b, hf):
                    dve.wait_ge(kv_hi_ready, 2 * b + hf + 1)
                    nc.vector.tensor_tensor(kv_lo[:, b, hf * HH:(hf + 1) * HH, :],
                                            ps_kv[:, hf, 0:HH * KVW].rearrange("p (h d) -> p h d", h=HH),
                                            kv_hi[:, b, hf * HH:(hf + 1) * HH, :], ALU.subtract).then_inc(kv_lo_ready, 1)

                def batch(b, first, last):
                    for t in range(TPB):
                        n = TPB * b + t
                        halves(n, t, 0, first)
                        if t == 1 and not first:
                            store_kv(b - 1, 1)
                        if not (last and t >= TPB - 1):
                            low_x(n + 1, (t + 1) % TPB)
                        if not (last and t >= TPB - 2):
                            normalize(n + 2)
                        halves(n, t, 1, first)
                        if t == 0 and not first:
                            store_kv(b - 1, 0)

                for t_, v in ((v_hi, 1.0), (v_lo, 0.0)):
                    for m in range(4):
                        nc.vector.memset(t_[:, m, :, DH:KVW], v).then_inc(ones_set, 1)
                normalize(0)
                low_x(0, 0)
                normalize(1)
                batch(0, True, False)
                with dve.Fori(1, BATCH - 1) as b:
                    batch(b, False, False)
                batch(BATCH - 1, False, True)
                store_kv(BATCH - 1, 0)
                store_kv(BATCH - 1, 1)

            @block.gpsimd
            def _(pool):
                def batch(b, first):
                    for t in range(TPB):
                        n = TPB * b + t
                        for hf in range(2):
                            m = KBUF[2 * t + hf]
                            pool.wait_ge(kf_hi_ready, 2 * n + hf + 1)
                            if not (first and 2 * t + hf < 3):
                                pool.wait_ge(summed, 2 * n + hf - 2)
                            nc.gpsimd.tensor_tensor(kf_lo[:, m, :, 0, :], kf[:, hf, :, 0, :], kf_hi[:, m, :, 0, :],
                                                    ALU.subtract).then_inc(kpos_lo_ready, 1)
                            if t < PER_BATCH:
                                c = PER_BATCH * b + t
                                cols = slice(hf * HC, (hf + 1) * HC)
                                pool.wait_ge(wf_hi_ready, c + 1)
                                last = nc.gpsimd.tensor_tensor(w['wf_lo'][:, c, cols], wf_f[:, t % 2, cols],
                                                               w['wf_hi'][:, c, cols], ALU.subtract)
                                if hf == 1:
                                    last.then_inc(wf_lo_ready, 1)

                batch(0, True)
                with pool.Fori(1, BATCH) as b:
                    batch(b, False)


def attend(nc, w, shared, kv_hi, kv_lo, stats, h, ident):
    OCT, QUAD = 8, 4
    NO, NQ = GH // OCT, GH // QUAD
    OC, QC = OCT * DH, QUAD * DH
    FC = INNER // P
    HC = INNER // 2
    RING = 3
    with ExitStack() as ctx:
        def sb(name, shape, dt):
            return ctx.enter_context(nc.sbuf_tensor(name, shape, dt))

        def sem(name):
            return ctx.enter_context(nc.semaphore(name))

        flat = shared[:, :, :].rearrange("p a b -> p (a b)")
        q = flat[:, 0:RING * OC].rearrange("p (r h d) -> p r h d", r=RING, h=OCT)
        y = flat[:, RING * OC:RING * OC + INNER]
        ys = flat[:, RING * OC + INNER:RING * OC + 2 * INNER]
        xn = sb("xn3", [P, 2 * P], F32)
        xh = sb("xh3", [P, 2, P], BF16)
        xl = sb("xl3", [P, P], BF16)
        xe = sb("xe3", [P, P], BF16)
        sq = sb("sq", [P, 2, OCT, DH], F32)
        z = sb("z", [P, 2, OCT, 2, DH], F32)
        phi = sb("phi", [P, 2, QUAD * P], F32)
        phi_hi = sb("phi_hi", [P, 2, QUAD * P], BF16)
        phi_lo = sb("phi_lo", [P, 2, QUAD * P], BF16)
        o = sb("o", [P, 2, QC], F32)
        o_hi = sb("o_hi", [P, 2, QC], BF16)
        o_lo = sb("o_lo", [P, 2, QC], BF16)
        ys_hi = sb("ys_hi", [P, INNER], BF16)
        ys_lo = sb("ys_lo", [P, INNER], BF16)
        mean = sb("q_mean", [P, 2, OCT], F32)
        ssq = sb("q_ssq", [P, 2, OCT], F32)
        den = sb("den", [P, 2, QUAD], F32)
        rec = sb("rec", [P, 2, QUAD], F32)
        bn = sb("y_bn", [P, 2, 6], F32)
        yst = sb("y_stats", [P, 2], F32)

        ps_a = ctx.enter_context(nc.psum_tensor("ps_a", [P, 2, 512], F32))
        ps_t = ctx.enter_context(nc.psum_tensor("ps_t3", [P, 2, 512], F32))
        ps_o = ctx.enter_context(nc.psum_tensor("ps_o", [P, 512], F32))
        ps_u = ctx.enter_context(nc.psum_tensor("ps_u", [P, 512], F32))
        ps_y = ctx.enter_context(nc.psum_tensor("ps_y", [P, 2, 512], F32))

        names = ("xe_zero xe_one x_norm x_turned xh_ready xe_ready xl_ready "
                 "queries gelu_done q_sum q_mean_s centered squared q_ssq_s q_var q_rstd q_scaled q_twice "
                 "q_turned phi_done phi_hi_done phi_lo_done attended den_done rec_done o_done "
                 "o_turned o_hi_done o_lo_done fused y_moved y_bn_s y_aggr y_var y_rstd y_norm "
                 "y_turned ys_done ys_hi_done ys_lo_done out_proj h_part h_done").split()
        s = {n: sem("at_" + n) for n in names}
        USES = ("oct3", "oct4", "oct5", "x", "oct0", "oct1", "f0", "f1", "oct2", "r")
        bank = {n: k % 2 for k, n in enumerate(USES)}

        class Tile:
            def __init__(self, t):
                self.t = t
                self.real = not isinstance(t, int) or 0 <= t < TILES

            def next(self):
                return Tile(self.t + 1)

            def prev(self):
                return Tile(self.t - 1)

        def unit(tile, k, n):
            while k >= n:
                tile, k = tile.next(), k - n
            while k < 0:
                tile, k = tile.prev(), k + n
            return tile, k

        def quad_of(tile, slot, lag):
            return unit(tile, slot - lag, NQ)

        def octet_of(tile, slot, lag):
            return unit(tile, (slot - lag) // 2 + 3, NO)

        def count(tile, k, n):
            return n * tile.t + k + 1

        def earlier(tile, k, n, back):
            if isinstance(tile.t, int) and n * tile.t + k - back < 0:
                return None
            return n * tile.t + k + 1 - back

        def batch_of(t):
            if isinstance(t, int):
                return t // TPB
            return ((t * 52) >> 8).with_bounds(min_val=0, max_val=BATCH - 1)

        def all_slots(eng, slot):
            for k in range(4, NQ):
                slot(Tile(-1), k)
            for t in range(2):
                for k in range(NQ):
                    slot(Tile(t), k)
            with eng.Fori(2, TILES - 1) as t:
                for k in range(NQ):
                    slot(Tile(t), k)
            for k in range(NQ):
                slot(Tile(TILES - 1), k)
            for k in range(NQ):
                slot(Tile(TILES), k)

        def read_after(tile, use):
            if use.startswith("oct"):
                of = tile if int(use[3:]) >= 3 else tile.next()
                return of, [("gelu_done", int(use[3:]), NO)]
            if use == "x":
                return tile.next(), [("xe_ready", 0, 1), ("xl_ready", 0, 1)]
            return tile.prev(), [("h_part", 0, 1)] if use == "r" else [("ys_done", int(use[1:]), 2)]

        def free_bank(eng, tile, use):
            k = USES.index(use)
            while True:
                k -= 2
                if k < 0:
                    tile, k = tile.prev(), k + len(USES)
                if isinstance(tile.t, int) and tile.t < -1:
                    return
                of, reads = read_after(tile, USES[k])
                if of.real:
                    for name, unit_, n in reads:
                        eng.wait_ge(s[name], count(of, unit_, n))
                    return

        with nc.Block() as block:
            @block.tensor
            def _(pe):
                def queries(tile, j, use_tile):
                    if j == 0:
                        for n in ("xh_ready", "xl_ready", "xe_ready"):
                            pe.wait_ge(s[n], count(tile, 0, 1))
                        pe.wait_ge(s["xe_one"], 2)
                    free_bank(pe, use_tile, f"oct{j}")
                    out = ps_a[:, bank[f"oct{j}"], 0:OC]
                    cols = slice(j * OC, (j + 1) * OC)
                    nc.tensor.matmul(out, xh[:, 0], w['q_hi'][:, 0, cols], start=True, stop=False)
                    nc.tensor.matmul(out, xh[:, 0], w['q_lo'][:, 0, cols], start=False, stop=False)
                    nc.tensor.matmul(out, xl[:, :], w['q_hi'][:, 0, cols], start=False, stop=False)
                    nc.tensor.matmul(out, xh[:, 1], w['q_hi'][:, 1, cols], start=False, stop=False)
                    nc.tensor.matmul(out, xe[:, :], w['q_lo'][:, 1, cols], start=False,
                                     stop=True).then_inc(s["queries"], 1)

                def turn_x(tile, use_tile):
                    pe.wait_ge(s["x_norm"], count(tile, 0, 1))
                    free_bank(pe, use_tile, "x")
                    for k in range(2):
                        last = nc.tensor.transpose(ps_a[:, bank["x"], k * P:(k + 1) * P], xn[:, k * P:(k + 1) * P],
                                                   ident[:, :])
                    last.then_inc(s["x_turned"], 1)

                def turn_quad(tile, k):
                    pe.wait_ge(s["q_twice"], count(tile, k // 2, NO))
                    if (n := earlier(tile, k, NQ, 2)) is not None:
                        pe.wait_ge(s["phi_done"], n)
                    for i in range(QUAD):
                        last = nc.tensor.transpose(
                            ps_t[:, k % 2, i * P:(i + 1) * P],
                            z[:, (k // 2) % 2, QUAD * (k % 2) + i].rearrange("p s d -> p (s d)"), ident[:, :])
                    last.then_inc(s["q_turned"], 1)

                def attend_quad(tile, k):
                    pe.wait_ge(s["phi_hi_done"], count(tile, k, NQ))
                    pe.wait_ge(s["phi_lo_done"], count(tile, k, NQ))
                    if (n := earlier(tile, k, NQ, 1)) is not None:
                        pe.wait_ge(s["o_done"], n)
                    b = batch_of(tile.t)
                    for i in range(QUAD):
                        hd = (QUAD * k + i) % HEADS
                        out = ps_o[:, i * KVW:(i + 1) * KVW]
                        ph, pl = (v[:, k % 2, i * P:(i + 1) * P] for v in (phi_hi, phi_lo))
                        nc.tensor.matmul(out, ph, kv_hi[:, b, hd, :], start=i == 0, stop=False, skip_group_check=True)
                        nc.tensor.matmul(out, ph, kv_lo[:, b, hd, :], start=False, stop=False, skip_group_check=True)
                        last = nc.tensor.matmul(out, pl, kv_hi[:, b, hd, :], start=False, stop=i == QUAD - 1,
                                                skip_group_check=True)
                    last.then_inc(s["attended"], 1)

                def turn_outputs(tile, k):
                    pe.wait_ge(s["o_done"], count(tile, k, NQ))
                    if (n := earlier(tile, k, NQ, 1)) is not None:
                        pe.wait_ge(s["o_hi_done"], n)
                        pe.wait_ge(s["o_lo_done"], n)
                    for i in range(2):
                        last = nc.tensor.transpose(ps_u[:, i * P:(i + 1) * P], o[:, k % 2, i * P:(i + 1) * P], ident[:, :])
                    last.then_inc(s["o_turned"], 1)

                def fuse(tile, k):
                    pe.wait_ge(s["o_hi_done"], count(tile, k, NQ))
                    pe.wait_ge(s["o_lo_done"], count(tile, k, NQ))
                    if k == 0 and (n := earlier(tile, 0, 1, 1)) is not None:
                        pe.wait_ge(s["y_moved"], n)
                    for i in range(2):
                        c = 2 * k + i
                        oh, ol = (v[:, k % 2, i * P:(i + 1) * P] for v in (o_hi, o_lo))
                        for lhs, part in ((oh, 'wf_hi'), (oh, 'wf_lo'), (ol, 'wf_hi')):
                            for n in range(2):
                                last = nc.tensor.matmul(ps_y[:, n, 0:HC], lhs, w[part][:, c, n * HC:(n + 1) * HC],
                                                        start=c == 0 and lhs is oh and part == 'wf_hi',
                                                        stop=c == 2 * NQ - 1 and lhs is ol)
                    last.then_inc(s["fused"], 1)

                def turn_y(tile, use_tile):
                    pe.wait_ge(s["y_norm"], count(tile, 0, 1))
                    for n in range(2):
                        free_bank(pe, use_tile, f"f{n}")
                        for i in range(FC // 2):
                            c = n * FC // 2 + i
                            last = nc.tensor.transpose(ps_a[:, bank[f"f{n}"], i * P:(i + 1) * P],
                                                       y[:, c * P:(c + 1) * P], ident[:, :])
                        last.then_inc(s["y_turned"], 1)

                def project_out(tile, use_tile):
                    pe.wait_ge(s["ys_hi_done"], count(tile, 0, 1))
                    pe.wait_ge(s["ys_lo_done"], count(tile, 0, 1))
                    free_bank(pe, use_tile, "r")
                    for c in range(FC):
                        for v, part in ((ys_hi, 'wo_hi'), (ys_hi, 'wo_lo'), (ys_lo, 'wo_hi')):
                            last = nc.tensor.matmul(ps_a[:, bank["r"], 0:DIM], v[:, c * P:(c + 1) * P], w[part][:, c, :],
                                                    start=c == 0 and v is ys_hi and part == 'wo_hi',
                                                    stop=c == FC - 1 and v is ys_lo)
                    last.then_inc(s["out_proj"], 1)

                def slot(tile, k):
                    if k % 2 == 0:
                        of, j = octet_of(tile, k, 0)
                        if of.real:
                            queries(of, j, tile)
                    if k == 4 and tile.next().real:
                        turn_x(tile.next(), tile)
                    if tile.real:
                        turn_quad(tile, k)
                    if k == 8 and tile.prev().real:
                        turn_y(tile.prev(), tile)
                    of, kk = quad_of(tile, k, 2)
                    if of.real:
                        attend_quad(of, kk)
                    of, kk = quad_of(tile, k, 3)
                    if of.real:
                        turn_outputs(of, kk)
                    of, kk = quad_of(tile, k, 4)
                    if of.real:
                        fuse(of, kk)
                    if k == 11 and tile.prev().real:
                        project_out(tile.prev(), tile)

                all_slots(pe, slot)

            @block.scalar
            def _(act):
                def gelu(tile, j):
                    act.wait_ge(s["queries"], count(tile, j, NO))
                    if (n := earlier(tile, j, NO, RING)) is not None:
                        act.wait_ge(s["q_scaled"], n)
                    nc.scalar.activation(q[:, j % RING].rearrange("p h d -> p (h d)"), ps_a[:, bank[f"oct{j}"], 0:OC],
                                         ACT.Gelu).then_inc(s["gelu_done"], 1)

                def square(tile, j):
                    act.wait_ge(s["centered"], count(tile, j, NO))
                    if (n := earlier(tile, j, NO, 2)) is not None:
                        act.wait_ge(s["q_ssq_s"], n)
                    nc.scalar.activation(sq[:, j % 2], q[:, j % RING], ACT.Square, scale=DH ** -0.5).then_inc(s["squared"], 1)

                def features(tile, k):
                    act.wait_ge(s["q_turned"], count(tile, k, NQ))
                    if (n := earlier(tile, k, NQ, 2)) is not None:
                        act.wait_ge(s["phi_hi_done"], n)
                        act.wait_ge(s["phi_lo_done"], n)
                    g = QUAD * k // HEADS
                    nc.scalar.activation(phi[:, k % 2], ps_t[:, k % 2, :], ACT.Relu, bias=w['betat'][:, g:g + 1],
                                         scale=w['gt'][:, g:g + 1]).then_inc(s["phi_done"], 1)

                def high_outputs(tile, k):
                    act.wait_ge(s["o_turned"], count(tile, k, NQ))
                    if (n := earlier(tile, k, NQ, 2)) is not None:
                        act.wait_ge(s["fused"], n)
                    nc.scalar.activation(o_hi[:, k % 2], ps_u[:, 0:QC], ACT.Copy).then_inc(s["o_hi_done"], 1)

                def move_x(tile):
                    act.wait_ge(s["x_turned"], count(tile, 0, 1))
                    if (n := earlier(tile, 0, 1, 1)) is not None:
                        act.wait_ge(s["queries"], NO * n)
                        act.wait_ge(s["xl_ready"], n)
                    nc.scalar.activation(xh[:, :, :], ps_a[:, bank["x"], 0:2 * P].rearrange("p (k n) -> p k n", k=2),
                                         ACT.Copy).then_inc(s["xh_ready"], 1)
                    nc.scalar.activation(xe[0:TAIL, :], ps_a[0:TAIL, bank["x"], P:2 * P], ACT.Copy).then_inc(s["xe_ready"], 1)

                def fused_gelu(tile, n):
                    act.wait_ge(s["y_turned"], count(tile, n, 2))
                    if (m := earlier(tile, 0, 1, 1)) is not None:
                        act.wait_ge(s["ys_hi_done"], m)
                        act.wait_ge(s["ys_lo_done"], m)
                    for i in range(FC // 2):
                        c = n * FC // 2 + i
                        last = nc.scalar.activation(ys[:, c * P:(c + 1) * P], ps_a[:, bank[f"f{n}"], i * P:(i + 1) * P],
                                                    ACT.Gelu, bias=w['betaf'][:, c:c + 1], scale=w['gf'][:, c:c + 1])
                    last.then_inc(s["ys_done"], 1)

                def slot(tile, k):
                    if k % 2 == 0:
                        of, j = octet_of(tile, k, 0)
                        if of.real:
                            gelu(of, j)
                    if k == 4 and tile.next().real:
                        move_x(tile.next())
                    if tile.real:
                        features(tile, k)
                    of, kk = quad_of(tile, k, 3)
                    if of.real:
                        high_outputs(of, kk)
                    if k % 2 == 0:
                        of, j = octet_of(tile, k, 2)
                        if of.real:
                            square(of, j)
                    if k in (8, 9) and tile.prev().real:
                        fused_gelu(tile.prev(), k - 8)

                act.wait_ge(s["xe_zero"], 1)
                all_slots(act, slot)

            @block.vector
            def _(dve):
                def normalize_x(tile):
                    if (n := earlier(tile, 0, 1, 1)) is not None:
                        dve.wait_ge(s["x_turned"], n)
                    t = tile.t
                    for lo, a_, b_ in ((0, 0, DIM), (DIM, P, DIM)):
                        last = nc.vector.tensor_scalar(xn[:, lo:lo + b_ - a_], h[:, t, a_:b_], stats[:, t, 0:1],
                                                       stats[:, t, 1:2], ALU.subtract, ALU.mult)
                    last.then_inc(s["x_norm"], 1)

                def low_x(tile):
                    dve.wait_ge(s["xe_ready"], count(tile, 0, 1))
                    if (n := earlier(tile, 0, 1, 1)) is not None:
                        dve.wait_ge(s["queries"], NO * n)
                    nc.vector.tensor_tensor(xl[:, :], ps_a[:, bank["x"], 0:P], xh[:, 0, :], ALU.subtract)
                    nc.vector.tensor_tensor(xh[TAIL:P, 1, :], ps_a[TAIL:P, bank["x"], P:2 * P], xh[TAIL:P, 1, :],
                                            ALU.subtract).then_inc(s["xl_ready"], 1)

                def sum_q(tile, j):
                    dve.wait_ge(s["gelu_done"], count(tile, j, NO))
                    if (n := earlier(tile, j, NO, 2)) is not None:
                        dve.wait_ge(s["centered"], n)
                    nc.vector.tensor_reduce(mean[:, j % 2], q[:, j % RING], AX_X, ALU.add).then_inc(s["q_sum"], 1)
                    dve.wait_ge(s["q_sum"], count(tile, j, NO))
                    nc.vector.tensor_scalar(mean[:, j % 2], mean[:, j % 2], 1.0 / DH, None,
                                            ALU.mult).then_inc(s["q_mean_s"], 1)

                def center(tile, j):
                    dve.wait_ge(s["q_mean_s"], count(tile, j, NO))
                    nc.vector.tensor_tensor(q[:, j % RING], q[:, j % RING],
                                            mean[:, j % 2].unsqueeze(2).broadcast_to([P, OCT, DH]),
                                            ALU.subtract).then_inc(s["centered"], 1)

                def sum_squares(tile, j):
                    dve.wait_ge(s["squared"], count(tile, j, NO))
                    if (n := earlier(tile, j, NO, 2)) is not None:
                        dve.wait_ge(s["q_scaled"], n)
                    nc.vector.tensor_reduce(ssq[:, j % 2], sq[:, j % 2], AX_X, ALU.add).then_inc(s["q_ssq_s"], 1)

                def scale_q(tile, j):
                    dve.wait_ge(s["q_rstd"], count(tile, j, NO))
                    if (n := earlier(tile, j, NO, 2)) is not None:
                        dve.wait_ge(s["q_turned"], 2 * n)
                    nc.vector.tensor_tensor(z[:, j % 2, :, 0, :], q[:, j % RING],
                                            ssq[:, j % 2].unsqueeze(2).broadcast_to([P, OCT, DH]),
                                            ALU.mult).then_inc(s["q_scaled"], 1)

                def double_q(tile, j):
                    dve.wait_ge(s["q_scaled"], count(tile, j, NO))
                    nc.vector.tensor_copy(z[:, j % 2, :, 1, :], z[:, j % 2, :, 0, :]).then_inc(s["q_twice"], 1)

                def high_phi(tile, k):
                    dve.wait_ge(s["phi_done"], count(tile, k, NQ))
                    if (n := earlier(tile, k, NQ, 2)) is not None:
                        dve.wait_ge(s["attended"], n)
                    nc.vector.tensor_copy(phi_hi[:, k % 2], phi[:, k % 2]).then_inc(s["phi_hi_done"], 1)

                def divide(tile, k):
                    dve.wait_ge(s["attended"], count(tile, k, NQ))
                    if (n := earlier(tile, k, NQ, 2)) is not None:
                        dve.wait_ge(s["o_done"], n)
                    v = ps_o[:, 0:QUAD * KVW].rearrange("p (h d) -> p h d", h=QUAD)
                    nc.vector.tensor_scalar(den[:, k % 2].unsqueeze(2), v[:, :, DH:KVW], NORM_EPS, None,
                                            ALU.add).then_inc(s["den_done"], 1)
                    dve.wait_ge(s["den_done"], count(tile, k, NQ))
                    nc.vector.reciprocal(rec[:, k % 2], den[:, k % 2]).then_inc(s["rec_done"], 1)
                    dve.wait_ge(s["rec_done"], count(tile, k, NQ))
                    if (n := earlier(tile, k, NQ, 2)) is not None:
                        dve.wait_ge(s["o_turned"], n)
                    nc.vector.tensor_tensor(o[:, k % 2].rearrange("p (h d) -> p h d", h=QUAD), v[:, :, 0:DH],
                                            rec[:, k % 2].unsqueeze(2).broadcast_to([P, QUAD, DH]),
                                            ALU.mult).then_inc(s["o_done"], 1)

                def low_outputs(tile, k):
                    dve.wait_ge(s["o_hi_done"], count(tile, k, NQ))
                    if (n := earlier(tile, k, NQ, 2)) is not None:
                        dve.wait_ge(s["fused"], n)
                    nc.vector.tensor_tensor(o_lo[:, k % 2], ps_u[:, 0:QC], o_hi[:, k % 2],
                                            ALU.subtract).then_inc(s["o_lo_done"], 1)

                def move_y(tile):
                    dve.wait_ge(s["fused"], count(tile, NQ - 1, NQ))
                    if (n := earlier(tile, 0, 1, 1)) is not None:
                        dve.wait_ge(s["y_turned"], 2 * n)
                    nc.vector.tensor_tensor(y.rearrange("p (n c) -> p n c", n=2), ps_y[:, :, 0:HC],
                                            w['bf'][:, :].rearrange("p (n c) -> p n c", n=2),
                                            ALU.add).then_inc(s["y_moved"], 1)

                def y_stats(tile):
                    dve.wait_ge(s["y_moved"], count(tile, 0, 1))
                    for n in range(2):
                        last = nc.vector.bn_stats(bn[:, n, :], y[:, n * HC:(n + 1) * HC])
                    last.then_inc(s["y_bn_s"], 1)

                def y_aggregate(tile):
                    nc.vector.bn_aggr(yst[:, :], bn[:, :, :]).then_inc(s["y_aggr"], 1)

                def normalize_y(tile):
                    dve.wait_ge(s["y_rstd"], count(tile, 0, 1))
                    nc.vector.tensor_scalar(y, y, yst[:, 0:1], yst[:, 1:2], ALU.subtract, ALU.mult).then_inc(s["y_norm"], 1)

                def high_ys(tile):
                    dve.wait_ge(s["ys_done"], count(tile, 1, 2))
                    if (n := earlier(tile, 0, 1, 1)) is not None:
                        dve.wait_ge(s["out_proj"], n)
                    nc.vector.tensor_copy(ys_hi[:, :], ys).then_inc(s["ys_hi_done"], 1)

                def add_to_h(tile):
                    dve.wait_ge(s["out_proj"], count(tile, 0, 1))
                    t = tile.t
                    nc.vector.tensor_tensor(h[:, t, :], ps_a[:, bank["r"], 0:DIM], h[:, t, :], ALU.add).then_inc(s["h_part"], 1)
                    dve.wait_ge(s["h_part"], count(tile, 0, 1))
                    nc.vector.tensor_tensor(h[:, t, :], h[:, t, :], w['bo'][:, :], ALU.add).then_inc(s["h_done"], 1)

                def slot(tile, k):
                    prev, nxt = tile.prev(), tile.next()
                    if k == 4 and prev.real:
                        move_y(prev)
                    if k % 2 == 0:
                        for lag, what in ((4, scale_q), (2, center)):
                            of, j = octet_of(tile, k, lag)
                            if of.real:
                                what(of, j)
                    else:
                        for lag, what in ((5, double_q), (3, sum_squares), (1, sum_q)):
                            of, j = octet_of(tile, k, lag)
                            if of.real:
                                what(of, j)
                    if k == 6 and prev.real:
                        dve.wait_ge(s["y_bn_s"], count(prev, 0, 1))
                    if k == 4 and nxt.real:
                        low_x(nxt)
                    of, kk = quad_of(tile, k, 2)
                    if of.real:
                        divide(of, kk)
                    if k == 6 and prev.real:
                        y_aggregate(prev)
                    of, kk = quad_of(tile, k, 3)
                    if of.real:
                        low_outputs(of, kk)
                    if tile.real:
                        high_phi(tile, k)
                    if k == 5 and prev.real:
                        y_stats(prev)
                    if k == 7 and prev.real:
                        normalize_y(prev)
                    if k == 2 and nxt.real:
                        normalize_x(nxt)
                    if k == 10 and prev.real:
                        high_ys(prev)
                    if k == 0 and prev.prev().real:
                        add_to_h(prev.prev())

                normalize_x(Tile(0))
                all_slots(dve, slot)
                add_to_h(Tile(TILES - 1))

            @block.gpsimd
            def _(pool):
                def rstd_q(tile, j):
                    pool.wait_ge(s["q_ssq_s"], count(tile, j, NO))
                    nc.gpsimd.tensor_tensor(ssq[:, j % 2], ssq[:, j % 2], w['eps'][:, 0:OCT],
                                            ALU.add).then_inc(s["q_var"], 1)
                    pool.wait_ge(s["q_var"], count(tile, j, NO))
                    nc.gpsimd.tensor_tensor(ssq[:, j % 2], ssq[:, j % 2], w['half'][:, 0:OCT],
                                            ALU.pow).then_inc(s["q_rstd"], 1)

                def low_phi(tile, k):
                    pool.wait_ge(s["phi_hi_done"], count(tile, k, NQ))
                    if (n := earlier(tile, k, NQ, 2)) is not None:
                        pool.wait_ge(s["attended"], n)
                    nc.gpsimd.tensor_tensor(phi_lo[:, k % 2], phi[:, k % 2], phi_hi[:, k % 2],
                                            ALU.subtract).then_inc(s["phi_lo_done"], 1)

                def rstd_y(tile):
                    pool.wait_ge(s["y_aggr"], count(tile, 0, 1))
                    nc.gpsimd.tensor_tensor(yst[:, 1:2], yst[:, 1:2], w['eps'][:, 0:1], ALU.add).then_inc(s["y_var"], 1)
                    pool.wait_ge(s["y_var"], count(tile, 0, 1))
                    nc.gpsimd.tensor_tensor(yst[:, 1:2], yst[:, 1:2], w['half'][:, 0:1], ALU.pow).then_inc(s["y_rstd"], 1)

                def low_ys(tile):
                    pool.wait_ge(s["ys_hi_done"], count(tile, 0, 1))
                    if (n := earlier(tile, 0, 1, 1)) is not None:
                        pool.wait_ge(s["out_proj"], n)
                    nc.gpsimd.tensor_tensor(ys_lo[:, :], ys, ys_hi[:, :], ALU.subtract).then_inc(s["ys_lo_done"], 1)

                def slot(tile, k):
                    if k % 2 == 1:
                        of, j = octet_of(tile, k, 3)
                        if of.real:
                            rstd_q(of, j)
                    if k == 6 and tile.prev().real:
                        rstd_y(tile.prev())
                    if tile.real:
                        low_phi(tile, k)
                    if k == 10 and tile.prev().real:
                        low_ys(tile.prev())

                nc.gpsimd.memset(xe[:, :], 0.0).then_inc(s["xe_zero"], 1)
                pool.wait_ge(s["xe_zero"], 1)
                for row in (TAIL, 96):
                    nc.gpsimd.memset(xe[row:row + 1, :], 1.0).then_inc(s["xe_one"], 1)
                all_slots(pool, slot)


def soft_experts(nc, a, out, h, ident):
    with ExitStack() as ctx:
        def sb(name, shape, dt=F32):
            return ctx.enter_context(nc.sbuf_tensor(name, shape, dt))

        def sem(name):
            return ctx.enter_context(nc.semaphore("ff_" + name))

        sl = sb("slots", [P, 2, NP_])
        sl_sq = sb("slots_sq", [P, 2, NP_])
        sl_n = sb("slots_norm", [P, 2, SLOTP])
        scale = sb("slot_scale", [P, 1])
        half = sb("halves", [P, 2, NP_])
        eps = sb("eps4", [P, TPB])
        wd = sb("w_down", [P, 2, EXPERTS, HID])
        bd = sb("b_down", [HID, EXPERTS])
        wu = sb("w_up", [HID, EXPERTS, DIM])
        bu = sb("b_up", [P, 2, EXPERTS])
        bn = sb("bn4", [P, TPB, 6])
        st = sb("stats4", [P, 2, TPB, 2])
        root = sb("root", [P, 2, 2, TPB])
        fac = sb("fac", [P, 2, TPB])
        xn = sb("xn4", [P, 2, TPB, DIM])
        xa = sb("xa", [P, 2, NTOK])
        xb = sb("xb", [TAIL, 2, NTOK])
        top = sb("top", [NP_, 2, 1])
        ed = sb("ed", [NP_, 2, NTOK])
        rs = sb("rs", [NP_, 2, 1])
        dt_ = sb("dispatch", [P, 2, TPB, NP_])
        cmax = sb("cmax", [P, 2, TPB])
        cl = sb("combine", [P, 2, TPB, NP_])
        csum = sb("csum", [P, 2, TPB])
        ct = sb("ct", [NP_, BATCH, NTOK])
        xt = sb("xtilde", [P, 2, EXPERTS, BATCH, SLOTP])
        ht = sb("hidden", [HID, EXPERTS, BATCH * SLOTP])
        yt = sb("ytilde", [P, 2, BATCH, EXPERTS, SLOTP])
        yr = sb("yrows", [NP_, BATCH, DIM])
        params_in, const_set = sem("params_in"), sem("const_set")
        is0 = lambda v: isinstance(v, int) and v == 0

        names = ("sl_sq sl_sum sl_root sl_steps sl_ready stat aggr var root1 root2 fac_steps fac xnorm turned xa_ready "
                 "xb_ready lt lmax nmax exped rrec escaled lc cmax cshift cexp csum crec cready dturned dt_ready "
                 "xtilde xt_ready cturned ct_ready").split()
        s = {n: sem(n) for n in names}

        with ExitStack() as one:
            ps_x = one.enter_context(nc.psum_tensor("ps_x4", [P, 2, 512], F32))
            ps_l = one.enter_context(nc.psum_tensor("ps_l4", [P, 2, 512], F32))
            ps_c = one.enter_context(nc.psum_tensor("ps_c4", [P, 512], F32))
            ps_d = one.enter_context(nc.psum_tensor("ps_d4", [P, 512], F32))
            ps_ct = one.enter_context(nc.psum_tensor("ps_ct4", [P, 2, 512], F32))
            HT = NTOK // 2

            def batches(eng, fn):
                for u in range(2):
                    fn(u, u, False)
                with eng.Fori(1, BATCH // 2) as i:
                    for u in range(2):
                        fn(2 * i + u, u, True)

            with nc.Block() as block:
                @block.sync
                def _(sp):
                    for t, n in ((sl, 'slots'), (wd, 'w_down'), (bd, 'b_down'), (wu, 'w_up'), (bu, 'b_up')):
                        sp.dma_start(t[:], a[n]).then_inc(params_in, 16)
                    sp.dma_start(scale[:, :], a['scale'].partition_broadcast(P)).then_inc(params_in, 16)
                    sp.wait_ge(params_in, 96)

                @block.gpsimd
                def _(pool):
                    nc.gpsimd.memset(half[:, 0, :], -0.5).then_inc(const_set, 1)
                    nc.gpsimd.memset(half[:, 1, :], 0.5).then_inc(const_set, 1)
                    nc.gpsimd.memset(eps[:, :], LN_EPS).then_inc(const_set, 1)
                    pool.wait_ge(const_set, 3)

                    def slot_norm():
                        pool.wait_ge(s["sl_sum"], 1)
                        nc.gpsimd.tensor_tensor(sl_n[:, :, :].rearrange("p k q -> p (k q)"),
                                                sl_n[:, :, :].rearrange("p k q -> p (k q)"),
                                                half[:, 1, 0:2 * SLOTP], ALU.pow).then_inc(s["sl_root"], 1)

                    def roots(b, u, again):
                        pool.wait_ge(s["aggr"], TPB * (b + 1))
                        if again:
                            pool.wait_ge(s["fac"], b - 1)
                        nc.gpsimd.tensor_tensor(root[:, u, 0, :], st[:, u, :, 1], eps[:, :], ALU.add).then_inc(s["var"], 1)
                        pool.wait_ge(s["var"], b + 1)
                        nc.gpsimd.tensor_tensor(root[:, u, 0, :], root[:, u, 0, :], half[:, 0, 0:TPB],
                                                ALU.pow).then_inc(s["root1"], 1)
                        nc.gpsimd.tensor_tensor(root[:, u, 1, :], st[:, u, :, 1], half[:, 1, 0:TPB],
                                                ALU.pow).then_inc(s["root2"], 1)
                        if is0(b):
                            slot_norm()

                    batches(pool, roots)

                @block.vector
                def _(dve):
                    def slots_square():
                        dve.wait_ge(params_in, 96)
                        nc.vector.tensor_tensor(sl_sq[:, :, :], sl[:, :, :], sl[:, :, :], ALU.mult).then_inc(s["sl_sq"], 1)
                        dve.wait_ge(s["sl_sq"], 1)
                        nc.vector.tensor_reduce(sl_n[:, :, :], sl_sq[:, :, :].rearrange("p k (n q) -> p k q n", q=SLOTP),
                                                AX_X, ALU.add).then_inc(s["sl_sum"], 1)

                    def slots_scale():
                        dve.wait_ge(s["sl_root"], 1)
                        nc.vector.tensor_scalar(sl_n[:, :, :], sl_n[:, :, :], L2_EPS, None,
                                                ALU.add).then_inc(s["sl_steps"], 1)
                        dve.wait_ge(s["sl_steps"], 1)
                        nc.vector.reciprocal(sl_n[:, :, :], sl_n[:, :, :]).then_inc(s["sl_steps"], 1)
                        dve.wait_ge(s["sl_steps"], 2)
                        nc.vector.tensor_scalar(sl_n[:, :, :], sl_n[:, :, :], scale[:, 0:1], None,
                                                ALU.mult).then_inc(s["sl_steps"], 1)
                        dve.wait_ge(s["sl_steps"], 3)
                        for k in range(2):
                            v = sl[:, k, :].rearrange("p (n q) -> p n q", q=SLOTP)
                            nc.vector.tensor_tensor(v, v, sl_n[:, k, :].unsqueeze(1).broadcast_to([P, EXPERTS, SLOTP]),
                                                    ALU.mult).then_inc(s["sl_ready"], 1)

                    def stats(b, u, again):
                        if again:
                            dve.wait_ge(s["xnorm"], b - 1)
                        dve.wait_ge(const_set, 3)
                        for t in range(TPB):
                            if not is0(b):
                                dve.wait_ge(s["aggr"], TPB * (b - 1) + t + 1)
                            nc.vector.bn_stats(bn[:, t, :], h[:, TPB * b + t, :]).then_inc(s["stat"], 1)
                        dve.wait_ge(s["stat"], TPB * (b + 1))
                        nc.vector.memset(fac[:, u, :], 0.0)
                        for t in range(TPB):
                            nc.vector.bn_aggr(st[:, u, t, :], bn[:, t, :]).then_inc(s["aggr"], 1)

                    def normalize(b, u, again):
                        dve.wait_ge(s["root1"], b + 1)
                        dve.wait_ge(s["root2"], b + 1)
                        nc.vector.tensor_tensor(fac[:, u, :], root[:, u, 0, :], root[:, u, 1, :], ALU.mult).then_inc(s["fac_steps"], 1)
                        dve.wait_ge(s["fac_steps"], 3 * b + 1)
                        nc.vector.tensor_scalar(fac[:, u, :], fac[:, u, :], DIM ** 0.5, L2_EPS, ALU.mult,
                                                ALU.add).then_inc(s["fac_steps"], 1)
                        dve.wait_ge(s["fac_steps"], 3 * b + 2)
                        nc.vector.reciprocal(fac[:, u, :], fac[:, u, :]).then_inc(s["fac_steps"], 1)
                        dve.wait_ge(s["fac_steps"], 3 * b + 3)
                        nc.vector.tensor_tensor(fac[:, u, :], fac[:, u, :], root[:, u, 0, :], ALU.mult).then_inc(s["fac"], 1)
                        dve.wait_ge(s["fac"], b + 1)
                        if again:
                            dve.wait_ge(s["xtilde"], b - 1)
                            dve.wait_ge(s["turned"], TPB * (b - 1))
                        for t in range(TPB):
                            last = nc.vector.tensor_scalar(xn[:, u, t, :], h[:, TPB * b + t, :], st[:, u, t, 0:1],
                                                           fac[:, u, t:t + 1], ALU.subtract, ALU.mult)
                        last.then_inc(s["xnorm"], 1)

                    def dispatch_max(b, u, again):
                        dve.wait_ge(s["lt"], b + 1)
                        if again:
                            dve.wait_ge(s["exped"], b - 1)
                        nc.vector.tensor_reduce(top[:, u, :], ps_l[0:NP_, :, 0:HT], mybir.AxisListType.XY,
                                                ALU.max).then_inc(s["lmax"], 1)
                        dve.wait_ge(s["lmax"], b + 1)
                        nc.vector.tensor_scalar(top[:, u, :], top[:, u, :], -1.0, None, ALU.mult).then_inc(s["nmax"], 1)

                    def combine(b, u, again):
                        dve.wait_ge(s["lc"], b + 1)
                        if again:
                            dve.wait_ge(s["cturned"], b - 1)
                        lg = ps_c[:, 0:TPB * NP_].rearrange("p (t n) -> p t n", t=TPB)
                        nc.vector.tensor_reduce(cmax[:, u, :], lg, AX_X, ALU.max).then_inc(s["cmax"], 1)
                        dve.wait_ge(s["cmax"], b + 1)
                        nc.vector.tensor_tensor(cl[:, u], lg, cmax[:, u].unsqueeze(2).broadcast_to([P, TPB, NP_]),
                                                ALU.subtract).then_inc(s["cshift"], 1)

                    def combine_scale(b, u, again):
                        dve.wait_ge(s["cexp"], b + 1)
                        nc.vector.tensor_reduce(csum[:, u, :], cl[:, u], AX_X, ALU.add).then_inc(s["csum"], 1)
                        dve.wait_ge(s["csum"], b + 1)
                        nc.vector.reciprocal(csum[:, u, :], csum[:, u, :]).then_inc(s["crec"], 1)
                        dve.wait_ge(s["crec"], b + 1)
                        nc.vector.tensor_tensor(cl[:, u], cl[:, u], csum[:, u].unsqueeze(2).broadcast_to([P, TPB, NP_]),
                                                ALU.mult).then_inc(s["cready"], 1)

                    def dispatch_scale(b, u, again):
                        dve.wait_ge(s["exped"], b + 1)
                        nc.vector.reciprocal(rs[:, u, :], rs[:, u, :]).then_inc(s["rrec"], 1)
                        dve.wait_ge(s["rrec"], b + 1)
                        nc.vector.tensor_scalar(ed[:, u, :], ed[:, u, :], rs[:, u, :], None, ALU.mult).then_inc(s["escaled"], 1)

                    def dispatch_move(b, u, again):
                        dve.wait_ge(s["dturned"], b + 1)
                        if again:
                            dve.wait_ge(s["xtilde"], b - 1)
                        nc.vector.tensor_copy(dt_[:, u], ps_d[:, 0:TPB * NP_].rearrange("p (t n) -> p t n", t=TPB)
                                              ).then_inc(s["dt_ready"], 1)

                    def batch(b, u, again):
                        if not is0(b):
                            stats(b, u, again)
                        normalize(b, u, again)
                        if is0(b):
                            slots_scale()
                        dispatch_max(b, u, again)
                        combine(b, u, again)
                        dispatch_scale(b, u, again)
                        combine_scale(b, u, again)
                        dispatch_move(b, u, again)

                    stats(0, 0, False)
                    slots_square()
                    batches(dve, batch)

                @block.scalar
                def _(act):
                    def batch(b, u, again):
                        if again:
                            act.wait_ge(s["lt"], b - 1)
                            act.wait_ge(s["lc"], b - 1)
                        for t in range(TPB):
                            act.wait_ge(s["turned"], TPB * b + t + 1)
                            at = slice(t * P, (t + 1) * P)
                            k = (TPB * u + t) % 2
                            nc.scalar.activation(xa[:, u, at], ps_x[:, k, 0:P], ACT.Copy)
                            nc.scalar.activation(xb[:, u, at], ps_x[0:TAIL, k, P:2 * P], ACT.Copy).then_inc(s["xb_ready"], 1)
                        act.wait_ge(s["nmax"], b + 1)
                        if again:
                            act.wait_ge(s["dturned"], b - 1)
                            act.wait_ge(s["rrec"], b - 1)
                        nc.scalar.activation(ed[:, u, :].rearrange("p (k n) -> p k n", k=2), ps_l[0:NP_, :, 0:HT], ACT.Exp,
                                             bias=top[:, u, :], accum_out=rs[:, u, :]).then_inc(s["exped"], 1)
                        act.wait_ge(s["cshift"], b + 1)
                        nc.scalar.activation(cl[:, u], cl[:, u], ACT.Exp).then_inc(s["cexp"], 1)
                        act.wait_ge(s["cturned"], b + 1)
                        nc.scalar.activation(ct[:, b, :].rearrange("p (k n) -> p k n", k=2), ps_ct[0:NP_, :, 0:HT],
                                             ACT.Copy).then_inc(s["ct_ready"], 1)
                        act.wait_ge(s["xtilde"], b + 1)
                        for k, rows in enumerate((P, TAIL)):
                            last = nc.scalar.activation(
                                xt[0:rows, k, :, b, :],
                                ps_d[0:rows, 256 + k * NP_:256 + (k + 1) * NP_].rearrange("p (n q) -> p n q", n=EXPERTS),
                                ACT.Copy)
                        last.then_inc(s["xt_ready"], 1)

                    batches(act, batch)

                @block.tensor
                def _(pe):
                    def batch(b, u, again):
                        pe.wait_ge(s["xnorm"], b + 1)
                        for t in range(TPB):
                            k = (TPB * u + t) % 2
                            if not (is0(b) and t < 2):
                                pe.wait_ge(s["xb_ready"], TPB * b + t - 1)
                            nc.tensor.transpose(ps_x[:, k, 0:P], xn[:, u, t, 0:P], ident[:, :])
                            nc.tensor.transpose(ps_x[0:TAIL, k, P:2 * P], xn[:, u, t, P:DIM],
                                                ident[:, :]).then_inc(s["turned"], 1)
                        if is0(b):
                            pe.wait_ge(s["sl_ready"], 2)
                        else:
                            pe.wait_ge(s["exped"], b)
                        pe.wait_ge(s["xb_ready"], TPB * (b + 1))
                        for k in range(2):
                            o = ps_l[0:NP_, k, 0:HT]
                            at = slice(k * HT, (k + 1) * HT)
                            nc.tensor.matmul(o, sl[:, 0, :], xa[:, u, at], start=True, stop=False)
                            last = nc.tensor.matmul(o, sl[0:TAIL, 1, :], xb[:, u, at], start=False, stop=True)
                        last.then_inc(s["lt"], 1)
                        if not is0(b):
                            pe.wait_ge(s["cshift"], b)
                        for t in range(TPB):
                            o = ps_c[:, t * NP_:(t + 1) * NP_]
                            at = slice(t * P, (t + 1) * P)
                            nc.tensor.matmul(o, xa[:, u, at], sl[:, 0, :], start=True, stop=False)
                            last = nc.tensor.matmul(o, xb[:, u, at], sl[0:TAIL, 1, :], start=False, stop=True)
                        last.then_inc(s["lc"], 1)
                        pe.wait_ge(s["escaled"], b + 1)
                        if not is0(b):
                            pe.wait_ge(s["xt_ready"], b)
                        pe.wait_ge(s["cready"], b + 1)
                        if not is0(b):
                            pe.wait_ge(s["ct_ready"], b)
                        for t in range(TPB):
                            c0 = t * P
                            for lo, hi in ((c0, min(c0 + P, HT)), (max(c0, HT), c0 + P)):
                                if lo < hi:
                                    k = lo // HT
                                    last = nc.tensor.transpose(ps_ct[0:NP_, k, lo - k * HT:hi - k * HT],
                                                               cl[lo - c0:hi - c0, u, t, :], ident[lo - c0:hi - c0, lo - c0:hi - c0])
                        last.then_inc(s["cturned"], 1)
                        for t in range(TPB):
                            last = nc.tensor.transpose(ps_d[:, t * NP_:(t + 1) * NP_], ed[:, u, t * P:(t + 1) * P],
                                                       ident[0:NP_, 0:NP_])
                        last.then_inc(s["dturned"], 1)
                        pe.wait_ge(s["dt_ready"], b + 1)
                        for k, (c, rows) in enumerate(((0, P), (P, TAIL))):
                            for t in range(TPB):
                                last = nc.tensor.matmul(ps_d[0:rows, 256 + k * NP_:256 + (k + 1) * NP_],
                                                        xn[:, u, t, c:c + rows], dt_[:, u, t, :], start=t == 0,
                                                        stop=t == TPB - 1)
                        last.then_inc(s["xtilde"], 1)

                    batches(pe, batch)

        with ExitStack() as two:
            ps_h = two.enter_context(nc.psum_tensor("ps_h4", [P, 512], F32))
            ps_y = two.enter_context(nc.psum_tensor("ps_y4", [P, 2, 512], F32))
            ps_r = two.enter_context(nc.psum_tensor("ps_r4", [P, 2, 512], F32))
            ps_o = two.enter_context(nc.psum_tensor("ps_o4", [P, 3, 512], F32))
            down, hid, up, biased, yturned, yr_ready, mixed, added, out_done = (
                sem(n) for n in ("down", "hid", "up", "biased", "yturned", "yr_ready", "mixed", "added", "out_done"))
            BQ = BATCH * SLOTP
            GROUPS = [(0, 2), (2, 2), (4, 1)]

            with nc.Block() as block:
                @block.tensor
                def _(pe):
                    for n in range(EXPERTS):
                        o = ps_h[0:HID, n * BQ:(n + 1) * BQ]
                        nc.tensor.matmul(o, wd[:, 0, n, :], xt[:, 0, n].rearrange("p b q -> p (b q)"), start=True, stop=False)
                        nc.tensor.matmul(o, wd[0:TAIL, 1, n, :], xt[0:TAIL, 1, n].rearrange("p b q -> p (b q)"),
                                         start=False, stop=True).then_inc(down, 1)
                    pe.wait_ge(hid, EXPERTS)
                    for n in range(EXPERTS):
                        for k, (c, rows) in enumerate(((0, P), (P, TAIL))):
                            last = nc.tensor.matmul(ps_y[0:rows, k, n * BQ:(n + 1) * BQ], wu[:, n, c:c + rows], ht[:, n, :],
                                                    start=True, stop=True)
                    last.then_inc(up, 1)
                    pe.wait_ge(biased, 2)
                    for b in range(BATCH):
                        if b >= 2:
                            pe.wait_ge(yr_ready, b - 1)
                        for k, (c, rows) in enumerate(((0, P), (P, TAIL))):
                            last = nc.tensor.transpose(ps_r[0:NP_, b % 2, c:c + rows],
                                                       yt[0:rows, k, b].rearrange("p n q -> p (n q)"), ident[0:rows, 0:rows])
                        last.then_inc(yturned, 1)
                    for b in range(BATCH):
                        pe.wait_ge(yr_ready, b + 1)
                        for g, (t0, nt) in enumerate(GROUPS):
                            if b >= 1:
                                pe.wait_ge(added, 3 * (b - 1) + g + 1)
                            for t in range(nt):
                                last = nc.tensor.matmul(ps_o[:, g, t * DIM:(t + 1) * DIM],
                                                        ct[:, b, (t0 + t) * P:(t0 + t + 1) * P], yr[:, b, :],
                                                        start=True, stop=True)
                            last.then_inc(mixed, 1)

                @block.scalar
                def _(act):
                    for n in range(EXPERTS):
                        act.wait_ge(down, EXPERTS)
                        nc.scalar.activation(ht[:, n, :], ps_h[0:HID, n * BQ:(n + 1) * BQ], ACT.Gelu,
                                             bias=bd[:, n:n + 1]).then_inc(hid, 1)
                    for b in range(BATCH):
                        act.wait_ge(yturned, b + 1)
                        nc.scalar.activation(yr[:, b, :], ps_r[0:NP_, b % 2, 0:DIM], ACT.Copy).then_inc(yr_ready, 1)

                @block.vector
                def _(dve):
                    dve.wait_ge(up, 1)
                    for k, rows in enumerate((P, TAIL)):
                        nc.vector.tensor_tensor(
                            yt[0:rows, k].rearrange("p b n q -> p n b q"),
                            ps_y[0:rows, k, 0:EXPERTS * BQ].rearrange("p (n b q) -> p n b q", n=EXPERTS, b=BATCH),
                            bu[0:rows, k, :].unsqueeze(2).unsqueeze(3).broadcast_to([rows, EXPERTS, BATCH, SLOTP]),
                            ALU.add).then_inc(biased, 1)
                    for b in range(BATCH):
                        for g, (t0, nt) in enumerate(GROUPS):
                            dve.wait_ge(mixed, 3 * b + g + 1)
                            rows = h[:, TPB * b + t0:TPB * b + t0 + nt, :]
                            nc.vector.tensor_tensor(rows, ps_o[:, g, 0:nt * DIM].rearrange("p (t d) -> p t d", t=nt), rows,
                                                    ALU.add).then_inc(added, 1)

                @block.sync
                def _(sp):
                    for b in range(BATCH):
                        sp.wait_ge(added, 3 * (b + 1))
                        sp.dma_start(out[b].rearrange("(t p) d -> p t d", p=P),
                                     h[:, TPB * b:TPB * (b + 1), :]).then_inc(out_done, 16)
                    sp.wait_ge(out_done, 16 * BATCH)


def early_fusion_kernel(nc, a, out):
    with ExitStack() as ctx:
        def sb(name, shape, dt):
            return ctx.enter_context(nc.sbuf_tensor(name, shape, dt))

        h = sb("h", [P, TILES, DIM], F32)
        ident = sb("ident", [P, P], F32)
        tokenizer(nc, a['x'], a['txt'], a['bands'], a['tok_w'], h, ident)
        with ExitStack() as attn:
            def sa(name, shape, dt):
                return attn.enter_context(nc.sbuf_tensor(name, shape, dt))

            stats = sa("stats", [P, TILES, 2], F32)
            kv_hi = sa("kvs_hi", [P, BATCH, HEADS, KVW], BF16)
            kv_lo = sa("kvs_lo", [P, BATCH, HEADS, KVW], BF16)
            w = {'gt': sa("gt", [P, G], F32), 'betat': sa("betat", [P, G], F32), 'gf': sa("gf", [P, INNER // P], F32),
                 'betaf': sa("betaf", [P, INNER // P], F32), 'bf': sa("bf", [P, INNER], F32),
                 'eps': sa("eps", [P, 8], F32), 'bo': sa("bo", [P, DIM], F32), 'half': sa("half", [P, TILES], F32),
                 'q_hi': sa("q_hi", [P, 2, QCOLS], BF16), 'q_lo': sa("q_lo", [P, 2, QCOLS], BF16),
                 'wo_hi': sa("wo_hi", [P, INNER // P, DIM], BF16), 'wo_lo': sa("wo_lo", [P, INNER // P, DIM], BF16)}
            shared = sa("shared", [P, 2, 2 * INNER], F32)
            w['kv_hi'], w['kv_lo'] = (shared[:, n].bitcast(BF16).rearrange("p (k c) -> p k c", k=2) for n in range(2))
            attention_weights(nc, a, w, stats, h, ident)
            w['wf_hi'] = sa("wf_hi", [P, QCOLS // P, INNER], BF16)
            w['wf_lo'] = sa("wf_lo", [P, QCOLS // P, INNER], BF16)
            keys_and_values(nc, a, w, kv_hi, kv_lo, stats, h, ident)
            attend(nc, w, shared, kv_hi, kv_lo, stats, h, ident)
        soft_experts(nc, a, out, h, ident)


_OUTS = [((8, 640, 192), 'float32')]


def _layout(i):
    import numpy as _np

    f = {k: _np.asarray(v) for k, v in i.items()}
    q = COORDS - TAIL
    x = f['x'].reshape(BATCH, 2, HALF, COORDS).transpose(0, 1, 3, 2)
    x = _np.concatenate([x, x[:, :, q:]], axis=2).reshape(BATCH, 2, FULL + 1, P, HALF).transpose(0, 1, 3, 2, 4)
    t = f['L0_tok_W'].reshape(DIM, COORDS, 2, BANDS).transpose(2, 1, 3, 0)
    sines, cosines = (t[k, 0:q].reshape(FULL, P, BANDS, DIM).transpose(1, 2, 0, 3) for k in range(2))
    tail = t[:, q:].reshape(P, BANDS, 1, DIM)
    tok_w = _np.concatenate([sines, tail, cosines], axis=2)

    def tails(v):
        return _np.stack([v[0:P], _np.concatenate([v[P:], v[P:]])], axis=1)

    kv_w = tails(_np.concatenate([f['L0_attn_Wk'], f['L0_attn_Wv']], axis=1))
    wq = f['L0_attn_Wq'].reshape(G, DIM, HEADS // 2, P).transpose(3, 0, 2, 1).reshape(P, G * HEADS // 2, DIM)
    wq_t = _np.concatenate([wq, wq[:, :, P:]], axis=2)
    wt_diag = _np.zeros((P, G, P), f['L0_attn_Wt'].dtype)
    bias_rows = _np.zeros((P - TAIL, G, HEADS, DH), f['L0_attn_bt'].dtype)
    for k in range(2):
        wt_diag[k * DH:(k + 1) * DH, :, k * DH:(k + 1) * DH] = f['L0_attn_Wt'].transpose(1, 0, 2)
        bias_rows[32 * k] = f['L0_attn_bt'][:, None, :]

    def twice(v):
        return _np.concatenate([v.T, v.T])

    def columns(v):
        return v.reshape(-1, P).T

    return {
        'x': x, 'txt': f['txt'], 'bands': f['L0_tok_freq_bands'], 'tok_w': tok_w, 'kv_w': kv_w, 'wq_t': wq_t,
        'wt_diag': wt_diag, 'bias_rows': bias_rows.reshape(P - TAIL, QCOLS),
        'gt': twice(f['L0_attn_gt']), 'betat': twice(f['L0_attn_betat']),
        'wf': f['L0_attn_Wf'].reshape(QCOLS // P, P, INNER), 'bf': f['L0_attn_bf'],
        'gf': columns(f['L0_attn_gf']), 'betaf': columns(f['L0_attn_betaf']),
        'slots': tails(f['L0_ffn_slot_params'].reshape(DIM, NP_)), 'scale': f['L0_ffn_scale'].reshape(1),
        'w_down': tails(f['L0_ffn_W_down'].transpose(1, 0, 2)), 'b_down': f['L0_ffn_b_down'].T,
        'w_up': f['L0_ffn_W_up'].transpose(1, 0, 2), 'b_up': tails(f['L0_ffn_b_up'].T),
        'wo': f['L0_attn_Wo'].reshape(INNER // P, P, DIM).transpose(1, 0, 2), 'bo': f['L0_attn_bo'],
    }


def kernel(**inputs):
    import numpy as _np
    import concourse.bacc as _bacc
    from concourse import mybir as _mybir
    from concourse.bass_utils import run_bass_kernel_spmd as _run

    nc = _bacc.Bacc("TRN2", target_bir_lowering=False, num_devices=1)
    arrays, args = {}, {}
    for name, a in _layout(inputs).items():
        arrays[f"in_{name}_dram"] = _np.ascontiguousarray(a)
        args[name] = nc.dram_tensor(f"in_{name}_dram", a.shape, _mybir.dt.from_np(a.dtype), kind="ExternalInput").ap()
    shape, dtype = _OUTS[0]
    out = nc.dram_tensor("out_0_dram", shape, _mybir.dt.from_np(_np.dtype(dtype)), kind="ExternalOutput").ap()
    early_fusion_kernel(nc, args, out)
    r = _run(nc, [arrays], core_ids=[0])
    return r.results[0]["out_0_dram"]
```

```python
from contextlib import ExitStack

import concourse.bass as bass
from concourse import mybir

F32 = mybir.dt.float32
I32 = mybir.dt.int32
BF16 = mybir.dt.bfloat16
ALU = mybir.AluOpType
ACT = mybir.ActivationFunctionType
AX_X = mybir.AxisListType.X

P = 128
BATCH, NIMG, NTXT, DIM = 8, 512, 128, 192
NTOK = NIMG + NTXT
TPB = NTOK // P
TILES = BATCH * TPB
TAIL = DIM - P

BANDS = 6
COORDS = 3 * DIM
FULL = COORDS // P
SLOTS = 2 * FULL + 1
HALF = 256
ROUND = 1.5 * 2.0 ** 23
SIGN_BIT = -2 ** 31
TWO_PI = 6.283185307179586

HEADS, DH, G = 12, 64, 4
INNER = HEADS * DH
GH = G * HEADS
QCOLS = G * INNER
KVW = DH + 1
LN_EPS = 1e-5
NORM_EPS = 1e-6 * (2 * DH) ** 0.5

EXPERTS, SLOTP, HID = 8, 4, DIM // 8
NP_ = EXPERTS * SLOTP
L2_EPS = 1e-6


def tokenizer(nc, x, txt, bands, tok_w, h, ident, staging, later_weights):
    with ExitStack() as ctx:
        def sb(name, shape, dt):
            return ctx.enter_context(nc.sbuf_tensor(name, shape, dt))

        def sem(name):
            return ctx.enter_context(nc.semaphore(name))

        w_hi = sb("w_hi", [P, BANDS, SLOTS, DIM], BF16)
        w_lo = sb("w_lo", [P, BANDS, SLOTS, DIM], BF16)
        w_last = sb("w_last", [P, SLOTS, DIM], F32)
        WB = SLOTS * DIM
        w_f = [staging[:, i * WB:(i + 1) * WB].rearrange("p (s d) -> p s d", d=DIM) for i in range(BANDS - 1)]
        w_f.append(w_last[:, :, :])
        fr = sb("fr", [P, BANDS], F32)
        NCH = FULL + 1
        RING = 3
        xt = sb("xt", [P, 2, NCH, HALF], F32)
        quarter = sb("quarter", [P, 1], F32)
        near = sb("near", [P, NCH, HALF], F32)
        turns = sb("turns", [P, 2, SLOTS, HALF], F32)
        feat = sb("feat", [P, RING, SLOTS, HALF], F32)
        f_hi = sb("f_hi", [P, RING, SLOTS, HALF], BF16)
        f_lo = sb("f_lo", [P, RING, SLOTS, HALF], BF16)
        acc = ctx.enter_context(nc.psum_tensor("acc", [P, 2, 2, 512], F32))
        x_in = [sem(f"x_in{i}") for i in range(2)]
        w_in = [sem(f"w_in{i}") for i in range(BANDS)]
        bands_in, txt_in, later_in = sem("bands_in"), sem("txt_in"), sem("later_in")
        zeroed, ident_ready = sem("zeroed"), sem("ident_ready")
        w_hi_ready, w_lo_ready = sem("w_hi_ready"), sem("w_lo_ready")
        shifted = sem("shifted")
        rounded = sem("rounded")
        reduced = sem("reduced")
        cos_ready = sem("cos_ready")
        hi_ready = sem("f_hi_ready")
        sin_ready = sem("sin_ready")
        quarter_ready = sem("quarter_ready")
        lo_ready = sem("lo_ready")
        multiplied = sem("multiplied")
        h_ready = sem("h_ready")
        STEPS = 2 * BANDS

        with nc.Block() as block:
            @block.sync
            def _(sp):
                def load(b, u):
                    sp.dma_start(xt[:, u], x[b, u]).then_inc(x_in[u], 16)

                sp.dma_start(fr[:, :], bands.partition_broadcast(P)).then_inc(bands_in, 16)
                load(0, 0)
                for i in range(BANDS):
                    sp.dma_start(w_f[i], tok_w[:, i]).then_inc(w_in[i], 16)
                    if i == 0:
                        load(0, 1)
                for b in range(BATCH):
                    sp.dma_start(h[:, TPB * b + TPB - 1, :], txt[b]).then_inc(txt_in, 16)
                sp.wait_ge(w_lo_ready, BANDS)
                for tile, source in later_weights:
                    sp.dma_start(tile, source).then_inc(later_in, 16)
                with sp.Fori(1, BATCH) as b:
                    for u in range(2):
                        sp.wait_ge(reduced, BANDS * (2 * b + u - 1))
                        load(b, u)
                sp.wait_ge(txt_in, 16 * BATCH)
                sp.wait_ge(later_in, 16 * len(later_weights))

            @block.tensor
            def _(pe):
                def batch(b):
                    for u in range(2):
                        for i in range(BANDS):
                            s = STEPS * b + BANDS * u + i
                            pe.wait_ge(hi_ready, s + 1)
                            if isinstance(b, int) and u == 0:
                                pe.wait_ge(w_lo_ready, i + 1)
                            if i == 0 and not (isinstance(b, int) and b == 0):
                                pe.wait_ge(h_ready, 2 * b + u - 1)
                            for t in range(2):
                                for k in range(SLOTS):
                                    hi = f_hi[:, i % RING, k, t * P:(t + 1) * P]
                                    nc.tensor.matmul(acc[:, u, t, 0:DIM], hi, w_hi[:, i, k, :],
                                                     start=i == 0 and k == 0, stop=False)
                                    nc.tensor.matmul(acc[:, u, t, 0:DIM], hi, w_lo[:, i, k, :], start=False, stop=False)
                            pe.wait_ge(lo_ready, s + 1)
                            for t in range(2):
                                for k in range(SLOTS):
                                    lo = f_lo[:, i % RING, k, t * P:(t + 1) * P]
                                    last = nc.tensor.matmul(acc[:, u, t, 0:DIM], lo, w_hi[:, i, k, :], start=False,
                                                            stop=i == BANDS - 1 and k == SLOTS - 1)
                            last.then_inc(multiplied, 1)

                batch(0)
                with pe.Fori(1, BATCH) as b:
                    batch(b)

            @block.scalar
            def _(act):
                def store_h(b, u):
                    act.wait_ge(multiplied, STEPS * b + BANDS * (u + 1))
                    nc.scalar.activation(h[:, bass.ds(TPB * b + 2 * u, 2), :], acc[:, u, :, 0:DIM],
                                         ACT.Copy).then_inc(h_ready, 1)

                def batch(b, first_batch):
                    for u in range(2):
                        for i in range(BANDS):
                            if first_batch and u == 0:
                                act.wait_ge(w_in[i], 16)
                                nc.scalar.activation(w_hi[:, i], w_f[i], ACT.Copy).then_inc(w_hi_ready, 1)
                            s = STEPS * b + BANDS * u + i
                            early = first_batch and u == 0 and i < RING
                            act.wait_ge(cos_ready, s + 1)
                            if not early:
                                act.wait_ge(multiplied, s + 1 - RING)
                            nc.scalar.activation(f_hi[:, i % RING, 0:FULL], turns[:, i % 2, 0:FULL], ACT.Sin,
                                                 scale=TWO_PI)
                            nc.scalar.activation(f_hi[:, i % RING, FULL:SLOTS], turns[:, i % 2, FULL:SLOTS], ACT.Sin,
                                                 bias=quarter[:, 0:1], scale=TWO_PI).then_inc(hi_ready, 1)
                            if not early:
                                act.wait_ge(lo_ready, s + 1 - RING)
                            nc.scalar.activation(feat[:, i % RING, 0:FULL], turns[:, i % 2, 0:FULL], ACT.Sin,
                                                 scale=TWO_PI)
                            nc.scalar.activation(feat[:, i % RING, FULL:SLOTS], turns[:, i % 2, FULL:SLOTS], ACT.Sin,
                                                 bias=quarter[:, 0:1], scale=TWO_PI).then_inc(sin_ready, 1)
                            if i == 2 and not (first_batch and u == 0):
                                store_h(b + u - 1, 1 - u)

                act.wait_ge(quarter_ready, 1)
                batch(0, True)
                with act.Fori(1, BATCH) as b:
                    batch(b, False)
                store_h(BATCH - 1, 1)

            @block.vector
            def _(dve):
                def reduce(b, u, i, first):
                    s = STEPS * b + BANDS * u + i
                    f = fr[:, i:i + 1]
                    if i == 0:
                        dve.wait_ge(x_in[u], 16 * b + 16)
                    if not (first and s == 0):
                        dve.wait_ge(reduced, s)
                    nc.vector.tensor_scalar(near[:, :, :], xt[:, u], f, ROUND, ALU.mult, ALU.add).then_inc(shifted, 1)
                    dve.wait_ge(shifted, s + 1)
                    nc.vector.tensor_scalar(near[:, :, :], near[:, :, :], ROUND, None, ALU.subtract).then_inc(rounded, 1)
                    dve.wait_ge(rounded, s + 1)
                    if not (first and s < 2):
                        dve.wait_ge(sin_ready, s - 1)
                    nc.vector.scalar_tensor_tensor(
                        out=turns[:, i % 2, 0:NCH, :].rearrange("p c n -> p (c n)"),
                        in0=xt[:, u].rearrange("p c n -> p (c n)"), scalar=f,
                        in1=near[:, :, :].rearrange("p c n -> p (c n)"),
                        op0=ALU.mult, op1=ALU.subtract).then_inc(reduced, 1)
                    dve.wait_ge(reduced, s + 1)
                    bits = turns[:, i % 2].bitcast(I32)
                    nc.vector.tensor_scalar(bits[:, NCH:SLOTS, :], bits[:, 0:FULL, :], SIGN_BIT, None, ALU.bitwise_or)
                    nc.vector.tensor_scalar(bits[P - TAIL:P, FULL, :], bits[P - TAIL:P, FULL, :], SIGN_BIT, None,
                                            ALU.bitwise_or)
                    nc.vector.tensor_scalar(turns[0:P - TAIL, i % 2, FULL, :], turns[0:P - TAIL, i % 2, FULL, :],
                                            0.25, None, ALU.subtract).then_inc(cos_ready, 1)

                def batch(b, first, last_batch):
                    for u in range(2):
                        for i in range(BANDS):
                            if i < BANDS - 1:
                                reduce(b, u, i + 1, first)
                            elif u == 0:
                                reduce(b, 1, 0, first)
                            elif not last_batch:
                                reduce(b + 1, 0, 0, False)
                            if first and u == 0:
                                dve.wait_ge(w_hi_ready, i + 1)
                                nc.vector.tensor_tensor(w_lo[:, i], w_f[i], w_hi[:, i],
                                                        ALU.subtract).then_inc(w_lo_ready, 1)

                dve.wait_ge(bands_in, 16)
                nc.vector.memset(quarter[:, :], TWO_PI / 4).then_inc(quarter_ready, 1)
                reduce(0, 0, 0, True)
                batch(0, True, False)
                with dve.Fori(1, BATCH - 1) as b:
                    batch(b, False, False)
                batch(BATCH - 1, False, True)

            @block.gpsimd
            def _(pool):
                nc.gpsimd.memset(ident[:, :], 0.0).then_inc(zeroed, 1)
                pool.wait_ge(zeroed, 1)
                nc.gpsimd.affine_select(out=ident[:, :], in_=ident[:, :], compare_op=ALU.not_equal, fill=1.0,
                                        base=0, pattern=[[-1, P]], channel_multiplier=1).then_inc(ident_ready, 1)

                def batch(b, first):
                    for u in range(2):
                        for i in range(BANDS):
                            s = STEPS * b + BANDS * u + i
                            pool.wait_ge(sin_ready, s + 1)
                            pool.wait_ge(hi_ready, s + 1)
                            if not (first and s < RING):
                                pool.wait_ge(multiplied, s + 1 - RING)
                            nc.gpsimd.tensor_tensor(f_lo[:, i % RING], feat[:, i % RING], f_hi[:, i % RING],
                                                    ALU.subtract).then_inc(lo_ready, 1)

                batch(0, True)
                with pool.Fori(1, BATCH) as b:
                    batch(b, False)


def attention_weights(nc, a, w, wq_t, kv_f, stats, h, ident):
    with ExitStack() as ctx:
        def sb(name, shape, dt):
            return ctx.enter_context(nc.sbuf_tensor(name, shape, dt))

        def sem(name):
            return ctx.enter_context(nc.semaphore(name))

        wt = sb("wt_diag", [P, G, P], F32)
        bn = sb("bn", [P, 4, 6], F32)
        bias = sb("bias_rows", [P, QCOLS], F32)
        bias_rest = sb("bias_rest", [P, G, DH], F32)
        wo_f = sb("wo_f", [P, INNER // P, DIM], F32)
        ps_f = ctx.enter_context(nc.psum_tensor("ps_f", [P, 4, 512], F32))
        wt_in, bias_in, wo_in, small_in = (sem(n) for n in ("wt_in", "bias_in", "wo_in", "small_in"))
        halved, folded, fold_hi, fold_lo = sem("halved"), sem("folded"), sem("fold_hi"), sem("fold_lo")
        kv_hi_done, kv_lo_done, wo_hi_done, wo_lo_done = (sem(n) for n in (
            "kv_hi_done", "kv_lo_done", "wo_hi_done", "wo_lo_done"))
        bias_hi, bias_split, bias_lo, signs_done = sem("bias_hi"), sem("bias_split"), sem("bias_lo"), sem("signs_done")
        bn_done, mean_done, var_done, rstd_done = sem("bn_done"), sem("mean_done"), sem("var_done"), sem("rstd_done")
        eps_set = sem("eps_set")
        LOW = 96
        PAIRS = G * HEADS // 2

        with nc.Block() as block:
            @block.sync
            def _(sp):
                sp.dma_start(wt[:, :, :], a['wt_diag']).then_inc(wt_in, 16)
                sp.dma_start(bias[TAIL:P, :], a['bias_rows']).then_inc(bias_in, 16)
                sp.dma_start(wo_f[:, :, :], a['wo']).then_inc(wo_in, 16)

            @block.scalar
            def _(act):
                for n in ('gt', 'betat', 'gf', 'betaf'):
                    act.dma_start(w[n][:, :], a[n]).then_inc(small_in, 16)
                act.dma_start(w['bf'][:, :], a['bf'].partition_broadcast(P)).then_inc(small_in, 16)
                act.dma_start(w['bo'][:, :], a['bo'].partition_broadcast(P)).then_inc(small_in, 16)
                for u in range(PAIRS):
                    act.wait_ge(folded, u + 1)
                    nc.scalar.activation(w['q_hi'][:, :, u * P:(u + 1) * P],
                                         ps_f[:, u % 4, 0:2 * P].rearrange("p (n c) -> p n c", n=2),
                                         ACT.Copy).then_inc(fold_hi, 1)
                    if u == 2:
                        nc.scalar.activation(w['kv_hi'], kv_f, ACT.Copy).then_inc(kv_hi_done, 1)
                    if u == 8:
                        act.wait_ge(bias_in, 16)
                        nc.scalar.activation(w['q_lo'][TAIL:P, 1, :], bias[TAIL:P, :], ACT.Copy).then_inc(bias_hi, 1)
                    if u == 14:
                        act.wait_ge(bias_split, 1)
                        nc.scalar.activation(
                            w['q_lo'][LOW:LOW + 1, 1, :].rearrange("p (g h d) -> p g h d", g=G, h=HEADS),
                            bias_rest[LOW:LOW + 1].unsqueeze(2).broadcast_to([1, G, HEADS, DH]),
                            ACT.Copy).then_inc(bias_lo, 1)
                    if u == 4:
                        act.wait_ge(wo_in, 16)
                        nc.scalar.activation(w['wo_hi'][:, :, :], wo_f[:, :, :], ACT.Copy).then_inc(wo_hi_done, 1)
                act.wait_ge(small_in, 16 * 6)

            @block.gpsimd
            def _(pool):
                def rstd(k):
                    n = slice(k * PART, (k + 1) * PART)
                    pool.wait_ge(mean_done, (k + 1) * PART)
                    nc.gpsimd.tensor_tensor(stats[:, n, 1], stats[:, n, 1], eps, ALU.add).then_inc(var_done, 1)
                    pool.wait_ge(var_done, k + 1)
                    nc.gpsimd.tensor_tensor(stats[:, n, 1], stats[:, n, 1], w['half'][:, 0:PART],
                                            ALU.pow).then_inc(rstd_done, 1)

                PART = 8
                eps = w['eps'][:, 0:PART]
                nc.gpsimd.memset(w['half'][:, :], -0.5).then_inc(halved, 1)
                nc.gpsimd.memset(w['eps'][:, :], LN_EPS).then_inc(eps_set, 1)
                pool.wait_ge(halved, 1)
                pool.wait_ge(eps_set, 1)
                pool.wait_ge(kv_hi_done, 1)
                nc.gpsimd.tensor_tensor(w['kv_lo'], kv_f, w['kv_hi'], ALU.subtract).then_inc(kv_lo_done, 1)
                rstd(0)
                rstd(1)
                pool.wait_ge(wo_hi_done, 1)
                nc.gpsimd.tensor_tensor(w['wo_lo'][:, :, :], wo_f[:, :, :], w['wo_hi'][:, :, :],
                                        ALU.subtract).then_inc(wo_lo_done, 1)
                for k in range(2, TILES // PART):
                    rstd(k)
                pool.wait_ge(rstd_done, TILES // PART)

            @block.tensor
            def _(pe):
                pe.wait_ge(wt_in, 16)
                for u in range(PAIRS):
                    if u >= 4:
                        pe.wait_ge(fold_lo, u - 3)
                    for k in range(2):
                        last = nc.tensor.matmul(ps_f[:, u % 4, k * P:(k + 1) * P], wq_t[:, u, k * P:(k + 1) * P],
                                                wt[:, u // (HEADS // 2), :], start=True, stop=True)
                    last.then_inc(folded, 1)

            @block.vector
            def _(dve):
                def row_stats(n):
                    for k in range(n, n + 2):
                        if k >= 4:
                            dve.wait_ge(mean_done, k - 3)
                        nc.vector.bn_stats(bn[:, k % 4, :], h[:, k, :]).then_inc(bn_done, 1)
                    for k in range(n, n + 2):
                        dve.wait_ge(bn_done, k + 1)
                        nc.vector.bn_aggr(stats[:, k, :], bn[:, k % 4, :]).then_inc(mean_done, 1)

                for n in range(0, 8, 2):
                    row_stats(n)
                for u in range(PAIRS):
                    dve.wait_ge(fold_hi, u + 1)
                    cols = slice(u * P, (u + 1) * P)
                    src = ps_f[:, u % 4, 0:2 * P].rearrange("p (n c) -> p n c", n=2)
                    nc.vector.tensor_tensor(w['q_lo'][:, 0, cols], src[:, 0], w['q_hi'][:, 0, cols], ALU.subtract)
                    nc.vector.tensor_tensor(w['q_lo'][0:TAIL, 1, cols], src[0:TAIL, 1], w['q_hi'][0:TAIL, 1, cols],
                                            ALU.subtract).then_inc(fold_lo, 1)
                    if 8 + 2 * u < TILES:
                        row_stats(8 + 2 * u)
                    if u == 12:
                        dve.wait_ge(bias_hi, 1)
                        of_head = (v[LOW:LOW + 1].rearrange("p (g h d) -> p g h d", g=G, h=HEADS)[:, :, 0, :]
                                   for v in (bias[:, :], w['q_lo'][:, 1, :]))
                        nc.vector.tensor_tensor(bias_rest[LOW:LOW + 1], next(of_head), next(of_head),
                                                ALU.subtract).then_inc(bias_split, 1)
                dve.wait_ge(small_in, 16 * 6)
                for n in ('gt', 'betat'):
                    nc.vector.tensor_scalar(w[n][DH:P, :], w[n][DH:P, :], -1.0, None, ALU.mult).then_inc(signs_done, 1)


def keys_and_values(nc, a, w, kv_hi, kv_lo, stats, h, ident):
    HH = HEADS // 2
    HC = HH * DH
    WF_CHUNKS = QCOLS // P
    PER_BATCH = WF_CHUNKS // BATCH
    XBUF = (0, 1, 2, 0, 1)
    KBUF = (0, 1, 2, 0, 1, 2, 0, 1, 2, 3)
    with ExitStack() as ctx:
        def sb(name, shape, dt):
            return ctx.enter_context(nc.sbuf_tensor(name, shape, dt))

        def sem(name):
            return ctx.enter_context(nc.semaphore(name))

        xn = sb("xn", [P, 2 * P], F32)
        xh = sb("xh", [P, 3, 2, P], BF16)
        xl = sb("xl", [P, 3, P], BF16)
        kf = sb("kf", [P, 2, HH, 2, DH], F32)
        kf_hi = sb("kf_hi", [P, 4, HH, 2, DH], BF16)
        kf_lo = sb("kf_lo", [P, 4, HH, 2, DH], BF16)
        v_hi = sb("v_hi", [P, 4, HH, KVW], BF16)
        v_lo = sb("v_lo", [P, 4, HH, KVW], BF16)
        wf_f = sb("wf_f", [P, 2, INNER], F32)
        ps_x = ctx.enter_context(nc.psum_tensor("ps_x2", [P, 512], F32))
        ps_p = ctx.enter_context(nc.psum_tensor("ps_p", [P, 2, 2, 512], F32))
        ps_kv = ctx.enter_context(nc.psum_tensor("ps_kv", [P, 2, 512], F32))
        ones_set, x_norm, x_turned, xh_ready, xl_ready = (sem(n) for n in ("ones_set", "x_norm", "x_turned2", "xh_ready", "xl_ready"))
        projected, kf_ready, kf_hi_ready, kpos_lo_ready, kneg_lo_ready, v_hi_ready, v_lo_ready = (sem(n) for n in (
            "projected", "kf_ready", "kf_hi_ready", "kpos_lo_ready", "kneg_lo_ready", "v_hi_ready", "v_lo_ready"))
        summed, kv_hi_ready, kv_lo_ready = sem("summed"), sem("kv_hi_ready"), sem("kv_lo_ready")
        wf_in = [sem(f"wf_in{i}") for i in range(2)]
        wf_hi_ready, wf_lo_ready = sem("wf_hi_ready"), sem("wf_lo_ready")
        wf = a['wf']
        is0 = lambda v: isinstance(v, int) and v == 0

        with nc.Block() as block:
            @block.sync
            def _(sp):
                def load(b):
                    for k in range(PER_BATCH):
                        before = {0: 0, 1: -1, 2: 1}[k]
                        if not is0(b) or k == 2:
                            sp.wait_ge(wf_lo_ready, PER_BATCH * b + before)
                        sp.dma_start(wf_f[:, k % 2, :], wf[PER_BATCH * b + k]).then_inc(wf_in[k % 2], 16)
                load(0)
                with sp.Fori(1, BATCH) as b:
                    load(b)

            @block.tensor
            def _(pe):
                def turn_x(n):
                    pe.wait_ge(x_norm, n + 1)
                    if not is0(n):
                        pe.wait_ge(xh_ready, n)
                        pe.wait_ge(xl_ready, n)
                    for k in range(2):
                        last = nc.tensor.transpose(ps_x[:, k * P:(k + 1) * P], xn[:, k * P:(k + 1) * P], ident[:, :])
                    last.then_inc(x_turned, 1)

                def project(n, t, hf, early):
                    if hf == 0:
                        pe.wait_ge(xh_ready, n + 1)
                        pe.wait_ge(xl_ready, n + 1)
                    if not early:
                        pe.wait_ge(kf_ready, 2 * n + hf - 1)
                        pe.wait_ge(v_lo_ready, 2 * n + hf - 1)
                    x = XBUF[t]
                    for kv in range(2):
                        cols = slice(kv * INNER + hf * HC, kv * INNER + (hf + 1) * HC)
                        out = ps_p[:, hf, kv, 0:HC]
                        nc.tensor.matmul(out, xh[:, x, 0], w['kv_hi'][:, 0, cols], start=True, stop=False)
                        nc.tensor.matmul(out, xh[:, x, 0], w['kv_lo'][:, 0, cols], start=False, stop=False)
                        nc.tensor.matmul(out, xl[:, x], w['kv_hi'][:, 0, cols], start=False, stop=False)
                        nc.tensor.matmul(out, xh[:, x, 1], w['kv_hi'][:, 1, cols], start=False, stop=False)
                        last = nc.tensor.matmul(out, xh[0:TAIL, x, 1], w['kv_lo'][0:TAIL, 1, cols], start=False, stop=True)
                    last.then_inc(projected, 1)

                def accumulate(b, t, hf, first_batch):
                    for s in (kf_hi_ready, kpos_lo_ready, kneg_lo_ready, v_hi_ready, v_lo_ready):
                        pe.wait_ge(s, 2 * (TPB * b + t) + hf + 1)
                    if t == 0 and not first_batch:
                        pe.wait_ge(kv_lo_ready, 2 * b - 1 + hf)
                    m = KBUF[2 * t + hf]
                    for j in range(HH):
                        out = ps_kv[:, hf, j * KVW:(j + 1) * KVW]
                        ph = kf_hi[:, m, j].rearrange("p s d -> p (s d)")
                        pl = kf_lo[:, m, j].rearrange("p s d -> p (s d)")
                        nc.tensor.matmul(out, ph, v_hi[:, m, j, :], start=t == 0 and j == 0, stop=False,
                                         skip_group_check=True)
                        nc.tensor.matmul(out, ph, v_lo[:, m, j, :], start=False, stop=False, skip_group_check=True)
                        last = nc.tensor.matmul(out, pl, v_hi[:, m, j, :], start=False,
                                                stop=t == TPB - 1 and j == HH - 1, skip_group_check=True)
                    last.then_inc(summed, 1)

                def tile(b, t, first_batch, last_batch):
                    n = TPB * b + t
                    for hf in range(2):
                        project(n, t, hf, first_batch and t == 0)
                        if hf == 1 and not (last_batch and t >= TPB - 2):
                            turn_x(n + 2)
                        if t >= 1:
                            accumulate(b, t - 1, hf, first_batch)
                        elif not first_batch:
                            accumulate(b - 1, TPB - 1, hf, False)

                turn_x(0)
                turn_x(1)
                for t in range(TPB):
                    tile(0, t, True, False)
                with pe.Fori(1, BATCH - 1) as b:
                    for t in range(TPB):
                        tile(b, t, False, False)
                for t in range(TPB):
                    tile(BATCH - 1, t, False, True)
                for hf in range(2):
                    accumulate(BATCH - 1, TPB - 1, hf, False)

            @block.scalar
            def _(act):
                def move_x(n, t, early):
                    act.wait_ge(x_turned, n + 1)
                    if not early:
                        act.wait_ge(projected, 2 * n - 2)
                        act.wait_ge(xl_ready, n - 1)
                    nc.scalar.activation(xh[:, XBUF[t]], ps_x[:, 0:2 * P].rearrange("p (k n) -> p k n", k=2),
                                         ACT.Copy).then_inc(xh_ready, 1)

                def key_features(n, t, hf, early):
                    m = KBUF[2 * t + hf]
                    act.wait_ge(projected, 2 * n + hf + 1)
                    if not (early and t == 0):
                        act.wait_ge(kf_hi_ready, 2 * n + hf - 1)
                        act.wait_ge(kpos_lo_ready, 2 * n + hf - 1)
                        act.wait_ge(kneg_lo_ready, 2 * n + hf - 1)
                    src = ps_p[:, hf, 0, 0:HC].rearrange("p (h d) -> p h d", h=HH)
                    nc.scalar.activation(kf[:, hf, :, 0, :], src, ACT.Relu)
                    nc.scalar.activation(kf[:, hf, :, 1, :], src, ACT.Relu, scale=-1.0).then_inc(kf_ready, 1)
                    if not (early and 2 * t + hf < 3):
                        act.wait_ge(summed, 2 * n + hf - 2)
                    nc.scalar.activation(v_hi[:, m, :, 0:DH], ps_p[:, hf, 1, 0:HC].rearrange("p (h d) -> p h d", h=HH),
                                         ACT.Copy).then_inc(v_hi_ready, 1)

                def store_kv(b, hf):
                    act.wait_ge(summed, 2 * TPB * b + 2 * (TPB - 1) + hf + 1)
                    nc.scalar.activation(kv_hi[:, b, hf * HH:(hf + 1) * HH, :],
                                         ps_kv[:, hf, 0:HH * KVW].rearrange("p (h d) -> p h d", h=HH),
                                         ACT.Copy).then_inc(kv_hi_ready, 1)

                def batch(b, first, last):
                    for t in range(TPB):
                        n = TPB * b + t
                        key_features(n, t, 0, first)
                        if t == 1 and not first:
                            store_kv(b - 1, 1)
                        key_features(n, t, 1, first)
                        if not (last and t >= TPB - 2):
                            move_x(n + 2, (t + 2) % TPB, False)
                        if t == 0 and not first:
                            store_kv(b - 1, 0)
                        if t < PER_BATCH:
                            act.wait_ge(wf_in[t % 2], 16 * b + 16 if t == 1 else 32 * b + 8 * t + 16)
                            nc.scalar.activation(w['wf_hi'][:, PER_BATCH * b + t, :], wf_f[:, t % 2, :],
                                                 ACT.Copy).then_inc(wf_hi_ready, 1)

                act.wait_ge(ones_set, 8)
                move_x(0, 0, True)
                move_x(1, 1, True)
                batch(0, True, False)
                with act.Fori(1, BATCH - 1) as b:
                    batch(b, False, False)
                batch(BATCH - 1, False, True)
                store_kv(BATCH - 1, 0)
                store_kv(BATCH - 1, 1)

            @block.vector
            def _(dve):
                def normalize(n):
                    if not is0(n):
                        dve.wait_ge(x_turned, n)
                    nc.vector.tensor_scalar(xn[:, 0:DIM], h[:, n, :], stats[:, n, 0:1], stats[:, n, 1:2],
                                            ALU.subtract, ALU.mult)
                    nc.vector.tensor_scalar(xn[:, DIM:2 * P], h[:, n, P:DIM], stats[:, n, 0:1], stats[:, n, 1:2],
                                            ALU.subtract, ALU.mult).then_inc(x_norm, 1)

                def low_x(n, t):
                    x = XBUF[t]
                    dve.wait_ge(xh_ready, n + 1)
                    nc.vector.tensor_tensor(xl[:, x], ps_x[:, 0:P], xh[:, x, 0, :], ALU.subtract)
                    nc.vector.tensor_tensor(xh[TAIL:P, x, 1, :], ps_x[TAIL:P, P:2 * P], xh[TAIL:P, x, 1, :],
                                            ALU.subtract).then_inc(xl_ready, 1)

                def halves(n, t, hf, early):
                    m = KBUF[2 * t + hf]
                    dve.wait_ge(kf_ready, 2 * n + hf + 1)
                    if not (early and 2 * t + hf < 3):
                        dve.wait_ge(summed, 2 * n + hf - 2)
                    nc.vector.tensor_copy(kf_hi[:, m], kf[:, hf]).then_inc(kf_hi_ready, 1)
                    dve.wait_ge(kf_hi_ready, 2 * n + hf + 1)
                    nc.vector.tensor_tensor(kf_lo[:, m, :, 1, :], kf[:, hf, :, 1, :], kf_hi[:, m, :, 1, :],
                                            ALU.subtract).then_inc(kneg_lo_ready, 1)
                    dve.wait_ge(v_hi_ready, 2 * n + hf + 1)
                    nc.vector.tensor_tensor(v_lo[:, m, :, 0:DH], ps_p[:, hf, 1, 0:HC].rearrange("p (h d) -> p h d", h=HH),
                                            v_hi[:, m, :, 0:DH], ALU.subtract).then_inc(v_lo_ready, 1)

                def store_kv(b, hf):
                    dve.wait_ge(kv_hi_ready, 2 * b + hf + 1)
                    nc.vector.tensor_tensor(kv_lo[:, b, hf * HH:(hf + 1) * HH, :],
                                            ps_kv[:, hf, 0:HH * KVW].rearrange("p (h d) -> p h d", h=HH),
                                            kv_hi[:, b, hf * HH:(hf + 1) * HH, :], ALU.subtract).then_inc(kv_lo_ready, 1)

                def batch(b, first, last):
                    for t in range(TPB):
                        n = TPB * b + t
                        halves(n, t, 0, first)
                        if t == 1 and not first:
                            store_kv(b - 1, 1)
                        halves(n, t, 1, first)
                        if not (last and t >= TPB - 2):
                            low_x(n + 2, (t + 2) % TPB)
                        if not (last and t >= TPB - 3):
                            normalize(n + 3)
                        if t == 0 and not first:
                            store_kv(b - 1, 0)

                for t_, v in ((v_hi, 1.0), (v_lo, 0.0)):
                    for m in range(4):
                        nc.vector.memset(t_[:, m, :, DH:KVW], v).then_inc(ones_set, 1)
                normalize(0)
                low_x(0, 0)
                normalize(1)
                low_x(1, 1)
                normalize(2)
                batch(0, True, False)
                with dve.Fori(1, BATCH - 1) as b:
                    batch(b, False, False)
                batch(BATCH - 1, False, True)
                store_kv(BATCH - 1, 0)
                store_kv(BATCH - 1, 1)

            @block.gpsimd
            def _(pool):
                def batch(b, first):
                    for t in range(TPB):
                        n = TPB * b + t
                        for hf in range(2):
                            m = KBUF[2 * t + hf]
                            pool.wait_ge(kf_hi_ready, 2 * n + hf + 1)
                            if not (first and 2 * t + hf < 3):
                                pool.wait_ge(summed, 2 * n + hf - 2)
                            nc.gpsimd.tensor_tensor(kf_lo[:, m, :, 0, :], kf[:, hf, :, 0, :], kf_hi[:, m, :, 0, :],
                                                    ALU.subtract).then_inc(kpos_lo_ready, 1)
                            if t < PER_BATCH:
                                c = PER_BATCH * b + t
                                cols = slice(hf * HC, (hf + 1) * HC)
                                pool.wait_ge(wf_hi_ready, c + 1)
                                last = nc.gpsimd.tensor_tensor(w['wf_lo'][:, c, cols], wf_f[:, t % 2, cols],
                                                               w['wf_hi'][:, c, cols], ALU.subtract)
                                if hf == 1:
                                    last.then_inc(wf_lo_ready, 1)

                batch(0, True)
                with pool.Fori(1, BATCH) as b:
                    batch(b, False)


def attend(nc, w, shared, kv_hi, kv_lo, stats, h, ident):
    OCT, QUAD = 8, 4
    NO, NQ = GH // OCT, GH // QUAD
    OC, QC = OCT * DH, QUAD * DH
    FC = INNER // P
    HC = INNER // 2
    RING = 3
    with ExitStack() as ctx:
        def sb(name, shape, dt):
            return ctx.enter_context(nc.sbuf_tensor(name, shape, dt))

        def sem(name):
            return ctx.enter_context(nc.semaphore(name))

        flat = shared[:, :, :].rearrange("p a b -> p (a b)")
        q = flat[:, 0:RING * OC].rearrange("p (r h d) -> p r h d", r=RING, h=OCT)
        y = flat[:, RING * OC:RING * OC + INNER]
        ys = flat[:, RING * OC + INNER:RING * OC + 2 * INNER]
        xn = sb("xn3", [P, 2 * P], F32)
        xh = sb("xh3", [P, 2, P], BF16)
        xl = sb("xl3", [P, P], BF16)
        xe = sb("xe3", [P, P], BF16)
        sq = sb("sq", [P, 2, OCT, DH], F32)
        z = sb("z", [P, 2, OCT, 2, DH], F32)
        phi = sb("phi", [P, 2, QUAD * P], F32)
        phi_hi = sb("phi_hi", [P, 2, QUAD * P], BF16)
        phi_lo = sb("phi_lo", [P, 2, QUAD * P], BF16)
        o = sb("o", [P, 2, QC], F32)
        o_hi = sb("o_hi", [P, 2, QC], BF16)
        o_lo = sb("o_lo", [P, 2, QC], BF16)
        ys_hi = sb("ys_hi", [P, INNER], BF16)
        ys_lo = sb("ys_lo", [P, INNER], BF16)
        mean = sb("q_mean", [P, 2, OCT], F32)
        ssq = sb("q_ssq", [P, 2, OCT], F32)
        den = sb("den", [P, 2, QUAD], F32)
        rec = sb("rec", [P, 2, QUAD], F32)
        bn = sb("y_bn", [P, 2, 6], F32)
        yst = sb("y_stats", [P, 2], F32)

        ps_a = ctx.enter_context(nc.psum_tensor("ps_a", [P, 2, 512], F32))
        ps_t = ctx.enter_context(nc.psum_tensor("ps_t3", [P, 2, 512], F32))
        ps_o = ctx.enter_context(nc.psum_tensor("ps_o", [P, 512], F32))
        ps_u = ctx.enter_context(nc.psum_tensor("ps_u", [P, 512], F32))
        ps_y = ctx.enter_context(nc.psum_tensor("ps_y", [P, 2, 512], F32))

        names = ("xe_zero xe_one x_norm x_turned xh_ready xe_ready xl_ready "
                 "queries gelu_done q_sum q_mean_s centered squared q_ssq_s q_var q_rstd q_scaled q_twice "
                 "q_turned phi_done phi_hi_done phi_lo_done attended den_done rec_done o_done "
                 "o_turned o_hi_done o_lo_done fused y_moved y_bn_s y_aggr y_var y_rstd y_norm "
                 "y_turned ys_done ys_hi_done ys_lo_done out_proj h_part h_done").split()
        s = {n: sem("at_" + n) for n in names}
        USES = ("oct3", "oct4", "oct5", "x", "oct0", "oct1", "f0", "f1", "oct2", "r")
        bank = {n: k % 2 for k, n in enumerate(USES)}

        class Tile:
            def __init__(self, t):
                self.t = t
                self.real = not isinstance(t, int) or 0 <= t < TILES

            def next(self):
                return Tile(self.t + 1)

            def prev(self):
                return Tile(self.t - 1)

        def unit(tile, k, n):
            while k >= n:
                tile, k = tile.next(), k - n
            while k < 0:
                tile, k = tile.prev(), k + n
            return tile, k

        def quad_of(tile, slot, lag):
            return unit(tile, slot - lag, NQ)

        def octet_of(tile, slot, lag):
            return unit(tile, (slot - lag) // 2 + 3, NO)

        def count(tile, k, n):
            return n * tile.t + k + 1

        def earlier(tile, k, n, back):
            if isinstance(tile.t, int) and n * tile.t + k - back < 0:
                return None
            return n * tile.t + k + 1 - back

        def batch_of(t):
            if isinstance(t, int):
                return t // TPB
            return ((t * 52) >> 8).with_bounds(min_val=0, max_val=BATCH - 1)

        def all_slots(eng, slot):
            for k in range(4, NQ):
                slot(Tile(-1), k)
            for t in range(2):
                for k in range(NQ):
                    slot(Tile(t), k)
            with eng.Fori(2, TILES - 1) as t:
                for k in range(NQ):
                    slot(Tile(t), k)
            for k in range(NQ):
                slot(Tile(TILES - 1), k)
            for k in range(NQ):
                slot(Tile(TILES), k)

        def read_after(tile, use):
            if use.startswith("oct"):
                of = tile if int(use[3:]) >= 3 else tile.next()
                return of, [("gelu_done", int(use[3:]), NO)]
            if use == "x":
                return tile.next(), [("xe_ready", 0, 1), ("xl_ready", 0, 1)]
            return tile.prev(), [("h_part", 0, 1)] if use == "r" else [("ys_done", int(use[1:]), 2)]

        def free_bank(eng, tile, use):
            k = USES.index(use)
            while True:
                k -= 2
                if k < 0:
                    tile, k = tile.prev(), k + len(USES)
                if isinstance(tile.t, int) and tile.t < -1:
                    return
                of, reads = read_after(tile, USES[k])
                if of.real:
                    for name, unit_, n in reads:
                        eng.wait_ge(s[name], count(of, unit_, n))
                    return

        with nc.Block() as block:
            @block.tensor
            def _(pe):
                def queries(tile, j, use_tile):
                    if j == 0:
                        for n in ("xh_ready", "xl_ready", "xe_ready"):
                            pe.wait_ge(s[n], count(tile, 0, 1))
                        pe.wait_ge(s["xe_one"], 2)
                    free_bank(pe, use_tile, f"oct{j}")
                    out = ps_a[:, bank[f"oct{j}"], 0:OC]
                    cols = slice(j * OC, (j + 1) * OC)
                    nc.tensor.matmul(out, xh[:, 0], w['q_hi'][:, 0, cols], start=True, stop=False)
                    nc.tensor.matmul(out, xh[:, 0], w['q_lo'][:, 0, cols], start=False, stop=False)
                    nc.tensor.matmul(out, xl[:, :], w['q_hi'][:, 0, cols], start=False, stop=False)
                    nc.tensor.matmul(out, xh[:, 1], w['q_hi'][:, 1, cols], start=False, stop=False)
                    nc.tensor.matmul(out, xe[:, :], w['q_lo'][:, 1, cols], start=False,
                                     stop=True).then_inc(s["queries"], 1)

                def turn_x(tile, use_tile):
                    pe.wait_ge(s["x_norm"], count(tile, 0, 1))
                    free_bank(pe, use_tile, "x")
                    for k in range(2):
                        last = nc.tensor.transpose(ps_a[:, bank["x"], k * P:(k + 1) * P], xn[:, k * P:(k + 1) * P],
                                                   ident[:, :])
                    last.then_inc(s["x_turned"], 1)

                def turn_quad(tile, k):
                    pe.wait_ge(s["q_twice"], count(tile, k // 2, NO))
                    if (n := earlier(tile, k, NQ, 2)) is not None:
                        pe.wait_ge(s["phi_done"], n)
                    for i in range(QUAD):
                        last = nc.tensor.transpose(
                            ps_t[:, k % 2, i * P:(i + 1) * P],
                            z[:, (k // 2) % 2, QUAD * (k % 2) + i].rearrange("p s d -> p (s d)"), ident[:, :])
                    last.then_inc(s["q_turned"], 1)

                def attend_quad(tile, k):
                    pe.wait_ge(s["phi_hi_done"], count(tile, k, NQ))
                    pe.wait_ge(s["phi_lo_done"], count(tile, k, NQ))
                    if (n := earlier(tile, k, NQ, 1)) is not None:
                        pe.wait_ge(s["o_done"], n)
                    b = batch_of(tile.t)
                    for i in range(QUAD):
                        hd = (QUAD * k + i) % HEADS
                        out = ps_o[:, i * KVW:(i + 1) * KVW]
                        ph, pl = (v[:, k % 2, i * P:(i + 1) * P] for v in (phi_hi, phi_lo))
                        nc.tensor.matmul(out, ph, kv_hi[:, b, hd, :], start=i == 0, stop=False, skip_group_check=True)
                        nc.tensor.matmul(out, ph, kv_lo[:, b, hd, :], start=False, stop=False, skip_group_check=True)
                        last = nc.tensor.matmul(out, pl, kv_hi[:, b, hd, :], start=False, stop=i == QUAD - 1,
                                                skip_group_check=True)
                    last.then_inc(s["attended"], 1)

                def turn_outputs(tile, k):
                    pe.wait_ge(s["o_done"], count(tile, k, NQ))
                    if (n := earlier(tile, k, NQ, 1)) is not None:
                        pe.wait_ge(s["o_hi_done"], n)
                        pe.wait_ge(s["o_lo_done"], n)
                    for i in range(2):
                        last = nc.tensor.transpose(ps_u[:, i * P:(i + 1) * P], o[:, k % 2, i * P:(i + 1) * P], ident[:, :])
                    last.then_inc(s["o_turned"], 1)

                def fuse(tile, k):
                    pe.wait_ge(s["o_hi_done"], count(tile, k, NQ))
                    pe.wait_ge(s["o_lo_done"], count(tile, k, NQ))
                    if k == 0 and (n := earlier(tile, 0, 1, 1)) is not None:
                        pe.wait_ge(s["y_moved"], n)
                    for i in range(2):
                        c = 2 * k + i
                        oh, ol = (v[:, k % 2, i * P:(i + 1) * P] for v in (o_hi, o_lo))
                        for lhs, part in ((oh, 'wf_hi'), (oh, 'wf_lo'), (ol, 'wf_hi')):
                            for n in range(2):
                                last = nc.tensor.matmul(ps_y[:, n, 0:HC], lhs, w[part][:, c, n * HC:(n + 1) * HC],
                                                        start=c == 0 and lhs is oh and part == 'wf_hi',
                                                        stop=c == 2 * NQ - 1 and lhs is ol)
                    last.then_inc(s["fused"], 1)

                def turn_y(tile, use_tile):
                    pe.wait_ge(s["y_norm"], count(tile, 0, 1))
                    for n in range(2):
                        free_bank(pe, use_tile, f"f{n}")
                        for i in range(FC // 2):
                            c = n * FC // 2 + i
                            last = nc.tensor.transpose(ps_a[:, bank[f"f{n}"], i * P:(i + 1) * P],
                                                       y[:, c * P:(c + 1) * P], ident[:, :])
                        last.then_inc(s["y_turned"], 1)

                def project_out(tile, use_tile):
                    pe.wait_ge(s["ys_hi_done"], count(tile, 0, 1))
                    pe.wait_ge(s["ys_lo_done"], count(tile, 0, 1))
                    free_bank(pe, use_tile, "r")
                    for c in range(FC):
                        for v, part in ((ys_hi, 'wo_hi'), (ys_hi, 'wo_lo'), (ys_lo, 'wo_hi')):
                            last = nc.tensor.matmul(ps_a[:, bank["r"], 0:DIM], v[:, c * P:(c + 1) * P], w[part][:, c, :],
                                                    start=c == 0 and v is ys_hi and part == 'wo_hi',
                                                    stop=c == FC - 1 and v is ys_lo)
                    last.then_inc(s["out_proj"], 1)

                def slot(tile, k):
                    if k % 2 == 0:
                        of, j = octet_of(tile, k, 0)
                        if of.real:
                            queries(of, j, tile)
                    if k == 4 and tile.next().real:
                        turn_x(tile.next(), tile)
                    if tile.real:
                        turn_quad(tile, k)
                    if k == 8 and tile.prev().real:
                        turn_y(tile.prev(), tile)
                    of, kk = quad_of(tile, k, 2)
                    if of.real:
                        attend_quad(of, kk)
                    of, kk = quad_of(tile, k, 3)
                    if of.real:
                        turn_outputs(of, kk)
                    of, kk = quad_of(tile, k, 4)
                    if of.real:
                        fuse(of, kk)
                    if k == 11 and tile.prev().real:
                        project_out(tile.prev(), tile)

                all_slots(pe, slot)

            @block.scalar
            def _(act):
                def gelu(tile, j):
                    act.wait_ge(s["queries"], count(tile, j, NO))
                    if (n := earlier(tile, j, NO, RING)) is not None:
                        act.wait_ge(s["q_scaled"], n)
                    nc.scalar.activation(q[:, j % RING].rearrange("p h d -> p (h d)"), ps_a[:, bank[f"oct{j}"], 0:OC],
                                         ACT.Gelu).then_inc(s["gelu_done"], 1)

                def square(tile, j):
                    act.wait_ge(s["centered"], count(tile, j, NO))
                    if (n := earlier(tile, j, NO, 2)) is not None:
                        act.wait_ge(s["q_ssq_s"], n)
                    nc.scalar.activation(sq[:, j % 2], q[:, j % RING], ACT.Square, scale=DH ** -0.5).then_inc(s["squared"], 1)

                def features(tile, k):
                    act.wait_ge(s["q_turned"], count(tile, k, NQ))
                    if (n := earlier(tile, k, NQ, 2)) is not None:
                        act.wait_ge(s["phi_hi_done"], n)
                        act.wait_ge(s["phi_lo_done"], n)
                    g = QUAD * k // HEADS
                    nc.scalar.activation(phi[:, k % 2], ps_t[:, k % 2, :], ACT.Relu, bias=w['betat'][:, g:g + 1],
                                         scale=w['gt'][:, g:g + 1]).then_inc(s["phi_done"], 1)

                def high_outputs(tile, k):
                    act.wait_ge(s["o_turned"], count(tile, k, NQ))
                    if (n := earlier(tile, k, NQ, 2)) is not None:
                        act.wait_ge(s["fused"], n)
                    nc.scalar.activation(o_hi[:, k % 2], ps_u[:, 0:QC], ACT.Copy).then_inc(s["o_hi_done"], 1)

                def move_x(tile):
                    act.wait_ge(s["x_turned"], count(tile, 0, 1))
                    if (n := earlier(tile, 0, 1, 1)) is not None:
                        act.wait_ge(s["queries"], NO * n)
                        act.wait_ge(s["xl_ready"], n)
                    nc.scalar.activation(xh[:, :, :], ps_a[:, bank["x"], 0:2 * P].rearrange("p (k n) -> p k n", k=2),
                                         ACT.Copy).then_inc(s["xh_ready"], 1)
                    nc.scalar.activation(xe[0:TAIL, :], ps_a[0:TAIL, bank["x"], P:2 * P], ACT.Copy).then_inc(s["xe_ready"], 1)

                def fused_gelu(tile, n):
                    act.wait_ge(s["y_turned"], count(tile, n, 2))
                    if (m := earlier(tile, 0, 1, 1)) is not None:
                        act.wait_ge(s["ys_hi_done"], m)
                        act.wait_ge(s["ys_lo_done"], m)
                    for i in range(FC // 2):
                        c = n * FC // 2 + i
                        last = nc.scalar.activation(ys[:, c * P:(c + 1) * P], ps_a[:, bank[f"f{n}"], i * P:(i + 1) * P],
                                                    ACT.Gelu, bias=w['betaf'][:, c:c + 1], scale=w['gf'][:, c:c + 1])
                    last.then_inc(s["ys_done"], 1)

                def slot(tile, k):
                    if k % 2 == 0:
                        of, j = octet_of(tile, k, 0)
                        if of.real:
                            gelu(of, j)
                    if k == 4 and tile.next().real:
                        move_x(tile.next())
                    if tile.real:
                        features(tile, k)
                    of, kk = quad_of(tile, k, 3)
                    if of.real:
                        high_outputs(of, kk)
                    if k % 2 == 0:
                        of, j = octet_of(tile, k, 2)
                        if of.real:
                            square(of, j)
                    if k in (8, 9) and tile.prev().real:
                        fused_gelu(tile.prev(), k - 8)

                act.wait_ge(s["xe_zero"], 1)
                all_slots(act, slot)

            @block.vector
            def _(dve):
                def normalize_x(tile):
                    if (n := earlier(tile, 0, 1, 1)) is not None:
                        dve.wait_ge(s["x_turned"], n)
                    t = tile.t
                    for lo, a_, b_ in ((0, 0, DIM), (DIM, P, DIM)):
                        last = nc.vector.tensor_scalar(xn[:, lo:lo + b_ - a_], h[:, t, a_:b_], stats[:, t, 0:1],
                                                       stats[:, t, 1:2], ALU.subtract, ALU.mult)
                    last.then_inc(s["x_norm"], 1)

                def low_x(tile):
                    dve.wait_ge(s["xe_ready"], count(tile, 0, 1))
                    if (n := earlier(tile, 0, 1, 1)) is not None:
                        dve.wait_ge(s["queries"], NO * n)
                    nc.vector.tensor_tensor(xl[:, :], ps_a[:, bank["x"], 0:P], xh[:, 0, :], ALU.subtract)
                    nc.vector.tensor_tensor(xh[TAIL:P, 1, :], ps_a[TAIL:P, bank["x"], P:2 * P], xh[TAIL:P, 1, :],
                                            ALU.subtract).then_inc(s["xl_ready"], 1)

                def sum_q(tile, j):
                    dve.wait_ge(s["gelu_done"], count(tile, j, NO))
                    if (n := earlier(tile, j, NO, 2)) is not None:
                        dve.wait_ge(s["centered"], n)
                    nc.vector.tensor_reduce(mean[:, j % 2], q[:, j % RING], AX_X, ALU.add).then_inc(s["q_sum"], 1)
                    dve.wait_ge(s["q_sum"], count(tile, j, NO))
                    nc.vector.tensor_scalar(mean[:, j % 2], mean[:, j % 2], 1.0 / DH, None,
                                            ALU.mult).then_inc(s["q_mean_s"], 1)

                def center(tile, j):
                    dve.wait_ge(s["q_mean_s"], count(tile, j, NO))
                    nc.vector.tensor_tensor(q[:, j % RING], q[:, j % RING],
                                            mean[:, j % 2].unsqueeze(2).broadcast_to([P, OCT, DH]),
                                            ALU.subtract).then_inc(s["centered"], 1)

                def sum_squares(tile, j):
                    dve.wait_ge(s["squared"], count(tile, j, NO))
                    if (n := earlier(tile, j, NO, 2)) is not None:
                        dve.wait_ge(s["q_scaled"], n)
                    nc.vector.tensor_reduce(ssq[:, j % 2], sq[:, j % 2], AX_X, ALU.add).then_inc(s["q_ssq_s"], 1)

                def scale_q(tile, j):
                    dve.wait_ge(s["q_rstd"], count(tile, j, NO))
                    if (n := earlier(tile, j, NO, 2)) is not None:
                        dve.wait_ge(s["q_turned"], 2 * n)
                    nc.vector.tensor_tensor(z[:, j % 2, :, 0, :], q[:, j % RING],
                                            ssq[:, j % 2].unsqueeze(2).broadcast_to([P, OCT, DH]),
                                            ALU.mult).then_inc(s["q_scaled"], 1)

                def double_q(tile, j):
                    dve.wait_ge(s["q_scaled"], count(tile, j, NO))
                    nc.vector.tensor_copy(z[:, j % 2, :, 1, :], z[:, j % 2, :, 0, :]).then_inc(s["q_twice"], 1)

                def high_phi(tile, k):
                    dve.wait_ge(s["phi_done"], count(tile, k, NQ))
                    if (n := earlier(tile, k, NQ, 2)) is not None:
                        dve.wait_ge(s["attended"], n)
                    nc.vector.tensor_copy(phi_hi[:, k % 2], phi[:, k % 2]).then_inc(s["phi_hi_done"], 1)

                def divide(tile, k):
                    dve.wait_ge(s["attended"], count(tile, k, NQ))
                    if (n := earlier(tile, k, NQ, 2)) is not None:
                        dve.wait_ge(s["o_done"], n)
                    v = ps_o[:, 0:QUAD * KVW].rearrange("p (h d) -> p h d", h=QUAD)
                    nc.vector.tensor_scalar(den[:, k % 2].unsqueeze(2), v[:, :, DH:KVW], NORM_EPS, None,
                                            ALU.add).then_inc(s["den_done"], 1)
                    dve.wait_ge(s["den_done"], count(tile, k, NQ))
                    nc.vector.reciprocal(rec[:, k % 2], den[:, k % 2]).then_inc(s["rec_done"], 1)
                    dve.wait_ge(s["rec_done"], count(tile, k, NQ))
                    if (n := earlier(tile, k, NQ, 2)) is not None:
                        dve.wait_ge(s["o_turned"], n)
                    nc.vector.tensor_tensor(o[:, k % 2].rearrange("p (h d) -> p h d", h=QUAD), v[:, :, 0:DH],
                                            rec[:, k % 2].unsqueeze(2).broadcast_to([P, QUAD, DH]),
                                            ALU.mult).then_inc(s["o_done"], 1)

                def low_outputs(tile, k):
                    dve.wait_ge(s["o_hi_done"], count(tile, k, NQ))
                    if (n := earlier(tile, k, NQ, 2)) is not None:
                        dve.wait_ge(s["fused"], n)
                    nc.vector.tensor_tensor(o_lo[:, k % 2], ps_u[:, 0:QC], o_hi[:, k % 2],
                                            ALU.subtract).then_inc(s["o_lo_done"], 1)

                def move_y(tile):
                    dve.wait_ge(s["fused"], count(tile, NQ - 1, NQ))
                    if (n := earlier(tile, 0, 1, 1)) is not None:
                        dve.wait_ge(s["y_turned"], 2 * n)
                    nc.vector.tensor_tensor(y.rearrange("p (n c) -> p n c", n=2), ps_y[:, :, 0:HC],
                                            w['bf'][:, :].rearrange("p (n c) -> p n c", n=2),
                                            ALU.add).then_inc(s["y_moved"], 1)

                def y_stats(tile):
                    dve.wait_ge(s["y_moved"], count(tile, 0, 1))
                    for n in range(2):
                        last = nc.vector.bn_stats(bn[:, n, :], y[:, n * HC:(n + 1) * HC])
                    last.then_inc(s["y_bn_s"], 1)

                def y_aggregate(tile):
                    nc.vector.bn_aggr(yst[:, :], bn[:, :, :]).then_inc(s["y_aggr"], 1)

                def normalize_y(tile):
                    dve.wait_ge(s["y_rstd"], count(tile, 0, 1))
                    nc.vector.tensor_scalar(y, y, yst[:, 0:1], yst[:, 1:2], ALU.subtract, ALU.mult).then_inc(s["y_norm"], 1)

                def high_ys(tile):
                    dve.wait_ge(s["ys_done"], count(tile, 1, 2))
                    if (n := earlier(tile, 0, 1, 1)) is not None:
                        dve.wait_ge(s["out_proj"], n)
                    nc.vector.tensor_copy(ys_hi[:, :], ys).then_inc(s["ys_hi_done"], 1)

                def add_to_h(tile):
                    dve.wait_ge(s["out_proj"], count(tile, 0, 1))
                    t = tile.t
                    nc.vector.tensor_tensor(h[:, t, :], ps_a[:, bank["r"], 0:DIM], h[:, t, :], ALU.add).then_inc(s["h_part"], 1)
                    dve.wait_ge(s["h_part"], count(tile, 0, 1))
                    nc.vector.tensor_tensor(h[:, t, :], h[:, t, :], w['bo'][:, :], ALU.add).then_inc(s["h_done"], 1)

                def slot(tile, k):
                    prev, nxt = tile.prev(), tile.next()
                    if k == 4 and prev.real:
                        move_y(prev)
                    if k % 2 == 0:
                        for lag, what in ((4, scale_q), (2, center)):
                            of, j = octet_of(tile, k, lag)
                            if of.real:
                                what(of, j)
                    else:
                        for lag, what in ((5, double_q), (3, sum_squares), (1, sum_q)):
                            of, j = octet_of(tile, k, lag)
                            if of.real:
                                what(of, j)
                    if k == 6 and prev.real:
                        dve.wait_ge(s["y_bn_s"], count(prev, 0, 1))
                    if k == 4 and nxt.real:
                        low_x(nxt)
                    of, kk = quad_of(tile, k, 2)
                    if of.real:
                        divide(of, kk)
                    if k == 6 and prev.real:
                        y_aggregate(prev)
                    of, kk = quad_of(tile, k, 3)
                    if of.real:
                        low_outputs(of, kk)
                    if tile.real:
                        high_phi(tile, k)
                    if k == 5 and prev.real:
                        y_stats(prev)
                    if k == 7 and prev.real:
                        normalize_y(prev)
                    if k == 2 and nxt.real:
                        normalize_x(nxt)
                    if k == 10 and prev.real:
                        high_ys(prev)
                    if k == 0 and prev.prev().real:
                        add_to_h(prev.prev())

                normalize_x(Tile(0))
                all_slots(dve, slot)
                add_to_h(Tile(TILES - 1))

            @block.gpsimd
            def _(pool):
                def rstd_q(tile, j):
                    pool.wait_ge(s["q_ssq_s"], count(tile, j, NO))
                    nc.gpsimd.tensor_tensor(ssq[:, j % 2], ssq[:, j % 2], w['eps'][:, 0:OCT],
                                            ALU.add).then_inc(s["q_var"], 1)
                    pool.wait_ge(s["q_var"], count(tile, j, NO))
                    nc.gpsimd.tensor_tensor(ssq[:, j % 2], ssq[:, j % 2], w['half'][:, 0:OCT],
                                            ALU.pow).then_inc(s["q_rstd"], 1)

                def low_phi(tile, k):
                    pool.wait_ge(s["phi_hi_done"], count(tile, k, NQ))
                    if (n := earlier(tile, k, NQ, 2)) is not None:
                        pool.wait_ge(s["attended"], n)
                    nc.gpsimd.tensor_tensor(phi_lo[:, k % 2], phi[:, k % 2], phi_hi[:, k % 2],
                                            ALU.subtract).then_inc(s["phi_lo_done"], 1)

                def rstd_y(tile):
                    pool.wait_ge(s["y_aggr"], count(tile, 0, 1))
                    nc.gpsimd.tensor_tensor(yst[:, 1:2], yst[:, 1:2], w['eps'][:, 0:1], ALU.add).then_inc(s["y_var"], 1)
                    pool.wait_ge(s["y_var"], count(tile, 0, 1))
                    nc.gpsimd.tensor_tensor(yst[:, 1:2], yst[:, 1:2], w['half'][:, 0:1], ALU.pow).then_inc(s["y_rstd"], 1)

                def low_ys(tile):
                    pool.wait_ge(s["ys_hi_done"], count(tile, 0, 1))
                    if (n := earlier(tile, 0, 1, 1)) is not None:
                        pool.wait_ge(s["out_proj"], n)
                    nc.gpsimd.tensor_tensor(ys_lo[:, :], ys, ys_hi[:, :], ALU.subtract).then_inc(s["ys_lo_done"], 1)

                def slot(tile, k):
                    if k % 2 == 1:
                        of, j = octet_of(tile, k, 3)
                        if of.real:
                            rstd_q(of, j)
                    if k == 6 and tile.prev().real:
                        rstd_y(tile.prev())
                    if tile.real:
                        low_phi(tile, k)
                    if k == 10 and tile.prev().real:
                        low_ys(tile.prev())

                nc.gpsimd.memset(xe[:, :], 0.0).then_inc(s["xe_zero"], 1)
                pool.wait_ge(s["xe_zero"], 1)
                for row in (TAIL, 96):
                    nc.gpsimd.memset(xe[row:row + 1, :], 1.0).then_inc(s["xe_one"], 1)
                all_slots(pool, slot)


def soft_experts(nc, a, out, h, ident):
    with ExitStack() as ctx:
        def sb(name, shape, dt=F32):
            return ctx.enter_context(nc.sbuf_tensor(name, shape, dt))

        def sem(name):
            return ctx.enter_context(nc.semaphore("ff_" + name))

        sl = sb("slots", [P, 2, NP_])
        sl_sq = sb("slots_sq", [P, 2, NP_])
        sl_n = sb("slots_norm", [P, 2, SLOTP])
        scale = sb("slot_scale", [P, 1])
        half = sb("halves", [P, 2, NP_])
        eps = sb("eps4", [P, TPB])
        wd = sb("w_down", [P, 2, EXPERTS, HID])
        bd = sb("b_down", [HID, EXPERTS])
        wu = sb("w_up", [HID, EXPERTS, DIM])
        bu = sb("b_up", [P, 2, EXPERTS])
        bn = sb("bn4", [P, TPB, 6])
        st = sb("stats4", [P, 2, TPB, 2])
        root = sb("root", [P, 2, 2, TPB])
        fac = sb("fac", [P, 2, TPB])
        xn = sb("xn4", [P, 2, TPB, 2 * P])
        xh = sb("xh4", [P, 2, NTOK], BF16)
        xl = sb("xl4", [P, NTOK], BF16)
        sl_hi = sb("slots_hi", [P, 2, NP_], BF16)
        sl_lo = sb("slots_lo", [P, 2, NP_], BF16)
        logits = sb("logits", [NP_, NTOK])
        top = sb("top", [NP_, 2, 1])
        ed = sb("ed", [NP_, 2, NTOK])
        rs = sb("rs", [NP_, 2, 1])
        dt_ = sb("dispatch", [P, 2, TPB, NP_])
        cmax = sb("cmax", [P, 2, TPB])
        cl = sb("combine", [P, 2, TPB, NP_])
        csum = sb("csum", [P, 2, TPB])
        ct_hi = sb("ct_hi", [NP_, BATCH, NTOK], BF16)
        ct_lo = sb("ct_lo", [NP_, BATCH, NTOK], BF16)
        xr = sb("xtilde_rows", [NP_, BATCH, DIM])
        xt = sb("xtilde", [P, 2, EXPERTS, BATCH, SLOTP])
        ht = sb("hidden", [HID, EXPERTS, BATCH * SLOTP])
        yt = sb("ytilde", [P, 2, BATCH, EXPERTS, SLOTP])
        yr_hi = sb("yrows_hi", [NP_, BATCH, DIM], BF16)
        yr_lo = sb("yrows_lo", [NP_, BATCH, DIM], BF16)
        params_in, const_set = sem("params_in"), sem("const_set")

        names = ("sl_sum sl_root sl_steps sl_ready sl_split stat aggr var root1 root2 fac_steps fac xnorm turned "
                 "xh_ready xl_ready lt lt_moved lmax nmax exped rrec escaled lc cmax cshift cexp csum_steps cready dturned dt_ready "
                 "xtilde xt_ready cturned ct_hi_ready ct_lo_ready").split()
        s = {n: sem(n) for n in names}

        with ExitStack() as one:
            ps_x = one.enter_context(nc.psum_tensor("ps_x4", [P, 2, 512], F32))
            ps_l = one.enter_context(nc.psum_tensor("ps_l4", [P, 2, 512], F32))
            ps_c = one.enter_context(nc.psum_tensor("ps_c4", [P, 512], F32))
            ps_d = one.enter_context(nc.psum_tensor("ps_d4", [P, 512], F32))
            ps_ct = one.enter_context(nc.psum_tensor("ps_ct4", [P, 2, 512], F32))
            HT = NTOK // 2

            def rounds(eng, fn):
                for b in range(2):
                    fn(b, b)
                with eng.Fori(1, BATCH // 2 - 1) as i:
                    for u in range(2):
                        fn(2 * i + u, u)
                for b in range(BATCH - 2, BATCH + 1):
                    fn(b, b % 2)

            def real(b):
                return not isinstance(b, int) or 0 <= b < BATCH

            def later(b, n):
                return not isinstance(b, int) or b >= n

            with nc.Block() as block:
                @block.sync
                def _(sp):
                    for t, n in ((sl, 'slots'), (wd, 'w_down'), (bd, 'b_down'), (wu, 'w_up'), (bu, 'b_up')):
                        sp.dma_start(t[:], a[n]).then_inc(params_in, 16)
                    sp.dma_start(scale[:, :], a['scale'].partition_broadcast(P)).then_inc(params_in, 16)
                    sp.wait_ge(params_in, 96)

                @block.gpsimd
                def _(pool):
                    nc.gpsimd.memset(half[:, 0, :], -0.5).then_inc(const_set, 1)
                    nc.gpsimd.memset(half[:, 1, :], 0.5).then_inc(const_set, 1)
                    nc.gpsimd.memset(eps[:, :], LN_EPS).then_inc(const_set, 1)
                    pool.wait_ge(const_set, 3)

                    def slot_norm():
                        pool.wait_ge(s["sl_sum"], 1)
                        nc.gpsimd.tensor_tensor(sl_n[:, :, :].rearrange("p k q -> p (k q)"),
                                                sl_n[:, :, :].rearrange("p k q -> p (k q)"),
                                                half[:, 1, 0:2 * SLOTP], ALU.pow).then_inc(s["sl_root"], 1)

                    def roots(b, u):
                        pool.wait_ge(s["aggr"], TPB * (b + 1))
                        if later(b, 2):
                            pool.wait_ge(s["fac"], b - 1)
                        nc.gpsimd.tensor_tensor(root[:, u, 0, :], st[:, u, :, 1], eps[:, :], ALU.add).then_inc(s["var"], 1)
                        pool.wait_ge(s["var"], b + 1)
                        nc.gpsimd.tensor_tensor(root[:, u, 0, :], root[:, u, 0, :], half[:, 0, 0:TPB],
                                                ALU.pow).then_inc(s["root1"], 1)
                        nc.gpsimd.tensor_tensor(root[:, u, 1, :], st[:, u, :, 1], half[:, 1, 0:TPB],
                                                ALU.pow).then_inc(s["root2"], 1)

                    def round_(b, u):
                        if real(b + 2):
                            roots(b + 2, u)

                    roots(0, 0)
                    roots(1, 1)
                    slot_norm()
                    rounds(pool, round_)

                @block.vector
                def _(dve):
                    def slots_square():
                        dve.wait_ge(params_in, 96)
                        nc.vector.tensor_tensor(sl_sq[:, :, :], sl[:, :, :], sl[:, :, :], ALU.mult).then_inc(s["sl_steps"], 1)
                        dve.wait_ge(s["sl_steps"], 1)
                        nc.vector.tensor_reduce(sl_n[:, :, :], sl_sq[:, :, :].rearrange("p k (n q) -> p k q n", q=SLOTP),
                                                AX_X, ALU.add).then_inc(s["sl_sum"], 1)

                    def slots_scale():
                        dve.wait_ge(s["sl_root"], 1)
                        nc.vector.tensor_scalar(sl_n[:, :, :], sl_n[:, :, :], L2_EPS, None,
                                                ALU.add).then_inc(s["sl_steps"], 1)
                        dve.wait_ge(s["sl_steps"], 2)
                        nc.vector.reciprocal(sl_n[:, :, :], sl_n[:, :, :]).then_inc(s["sl_steps"], 1)
                        dve.wait_ge(s["sl_steps"], 3)
                        nc.vector.tensor_scalar(sl_n[:, :, :], sl_n[:, :, :], scale[:, 0:1], None,
                                                ALU.mult).then_inc(s["sl_steps"], 1)
                        dve.wait_ge(s["sl_steps"], 4)
                        for k in range(2):
                            v = sl[:, k, :].rearrange("p (n q) -> p n q", q=SLOTP)
                            nc.vector.tensor_tensor(v, v, sl_n[:, k, :].unsqueeze(1).broadcast_to([P, EXPERTS, SLOTP]),
                                                    ALU.mult).then_inc(s["sl_ready"], 1)
                        dve.wait_ge(s["sl_ready"], 2)
                        nc.vector.tensor_copy(sl_hi[:, :, :], sl[:, :, :]).then_inc(s["sl_split"], 1)
                        dve.wait_ge(s["sl_split"], 1)
                        nc.vector.tensor_tensor(sl_lo[:, :, :], sl[:, :, :], sl_hi[:, :, :],
                                                ALU.subtract).then_inc(s["sl_split"], 1)

                    def stats(b, u):
                        if later(b, 2):
                            dve.wait_ge(s["xnorm"], b - 1)
                        dve.wait_ge(const_set, 3)
                        for t in range(TPB):
                            if later(b, 1):
                                dve.wait_ge(s["aggr"], TPB * (b - 1) + t + 1)
                            nc.vector.bn_stats(bn[:, t, :], h[:, TPB * b + t, :]).then_inc(s["stat"], 1)
                        dve.wait_ge(s["stat"], TPB * (b + 1))
                        nc.vector.memset(fac[:, u, :], 0.0)
                        for t in range(TPB):
                            nc.vector.bn_aggr(st[:, u, t, :], bn[:, t, :]).then_inc(s["aggr"], 1)

                    def normalize(b, u):
                        dve.wait_ge(s["root1"], b + 1)
                        dve.wait_ge(s["root2"], b + 1)
                        nc.vector.tensor_tensor(fac[:, u, :], root[:, u, 0, :], root[:, u, 1, :], ALU.mult).then_inc(s["fac_steps"], 1)
                        dve.wait_ge(s["fac_steps"], 3 * b + 1)
                        nc.vector.tensor_scalar(fac[:, u, :], fac[:, u, :], DIM ** 0.5, L2_EPS, ALU.mult,
                                                ALU.add).then_inc(s["fac_steps"], 1)
                        dve.wait_ge(s["fac_steps"], 3 * b + 2)
                        nc.vector.reciprocal(fac[:, u, :], fac[:, u, :]).then_inc(s["fac_steps"], 1)
                        dve.wait_ge(s["fac_steps"], 3 * b + 3)
                        nc.vector.tensor_tensor(fac[:, u, :], fac[:, u, :], root[:, u, 0, :], ALU.mult).then_inc(s["fac"], 1)
                        dve.wait_ge(s["fac"], b + 1)
                        if later(b, 2):
                            dve.wait_ge(s["xtilde"], b - 1)
                            dve.wait_ge(s["turned"], TPB * (b - 1))
                        for t in range(TPB):
                            nc.vector.tensor_scalar(xn[:, u, t, 0:DIM], h[:, TPB * b + t, :], st[:, u, t, 0:1],
                                                    fac[:, u, t:t + 1], ALU.subtract, ALU.mult)
                            last = nc.vector.tensor_scalar(xn[:, u, t, DIM:2 * P], h[:, TPB * b + t, P:DIM],
                                                           st[:, u, t, 0:1], fac[:, u, t:t + 1], ALU.subtract, ALU.mult)
                        last.then_inc(s["xnorm"], 1)

                    def low_x(b, u, tiles):
                        for t in tiles:
                            dve.wait_ge(s["xh_ready"], TPB * b + t + 1)
                            at = slice(t * P, (t + 1) * P)
                            k = (TPB * u + t) % 2
                            nc.vector.tensor_tensor(xl[:, at], ps_x[:, k, 0:P], xh[:, 0, at], ALU.subtract)
                            nc.vector.tensor_tensor(xh[TAIL:P, 1, at], ps_x[TAIL:P, k, P:2 * P], xh[TAIL:P, 1, at],
                                                    ALU.subtract).then_inc(s["xl_ready"], 1)

                    def dispatch_max(b, u):
                        dve.wait_ge(s["lt_moved"], b + 1)
                        if later(b, 2):
                            dve.wait_ge(s["exped"], b - 1)
                        nc.vector.tensor_reduce(top[:, u, :], ps_l[0:NP_, :, 0:HT], mybir.AxisListType.XY,
                                                ALU.max).then_inc(s["lmax"], 1)
                        dve.wait_ge(s["lmax"], b + 1)
                        nc.vector.tensor_scalar(top[:, u, :], top[:, u, :], -1.0, None, ALU.mult).then_inc(s["nmax"], 1)

                    def combine(b, u):
                        dve.wait_ge(s["lc"], b + 1)
                        if later(b, 2):
                            dve.wait_ge(s["cturned"], b - 1)
                        lg = ps_c[:, 0:TPB * NP_].rearrange("p (t n) -> p t n", t=TPB)
                        nc.vector.tensor_reduce(cmax[:, u, :], lg, AX_X, ALU.max).then_inc(s["cmax"], 1)
                        dve.wait_ge(s["cmax"], b + 1)
                        nc.vector.tensor_tensor(cl[:, u], lg, cmax[:, u].unsqueeze(2).broadcast_to([P, TPB, NP_]),
                                                ALU.subtract).then_inc(s["cshift"], 1)

                    def combine_scale(b, u):
                        dve.wait_ge(s["cexp"], b + 1)
                        nc.vector.tensor_reduce(csum[:, u, :], cl[:, u], AX_X, ALU.add).then_inc(s["csum_steps"], 1)
                        dve.wait_ge(s["csum_steps"], 2 * b + 1)
                        nc.vector.reciprocal(csum[:, u, :], csum[:, u, :]).then_inc(s["csum_steps"], 1)
                        dve.wait_ge(s["csum_steps"], 2 * b + 2)
                        nc.vector.tensor_tensor(cl[:, u], cl[:, u], csum[:, u].unsqueeze(2).broadcast_to([P, TPB, NP_]),
                                                ALU.mult).then_inc(s["cready"], 1)

                    def dispatch_scale(b, u):
                        dve.wait_ge(s["exped"], b + 1)
                        nc.vector.reciprocal(rs[:, u, :], rs[:, u, :]).then_inc(s["rrec"], 1)
                        dve.wait_ge(s["rrec"], b + 1)
                        nc.vector.tensor_scalar(ed[:, u, :], ed[:, u, :], rs[:, u, :], None, ALU.mult).then_inc(s["escaled"], 1)

                    def dispatch_move(b, u):
                        dve.wait_ge(s["dturned"], b + 1)
                        if later(b, 2):
                            dve.wait_ge(s["xtilde"], b - 1)
                        nc.vector.tensor_copy(dt_[:, u], ps_d[:, 0:TPB * NP_].rearrange("p (t n) -> p t n", t=TPB)
                                              ).then_inc(s["dt_ready"], 1)

                    def low_combine(b, u):
                        dve.wait_ge(s["ct_hi_ready"], b + 1)
                        nc.vector.tensor_tensor(ct_lo[:, b, :].rearrange("p (k n) -> p k n", k=2), ps_ct[0:NP_, :, 0:HT],
                                                ct_hi[:, b, :].rearrange("p (k n) -> p k n", k=2),
                                                ALU.subtract).then_inc(s["ct_lo_ready"], 1)

                    def round_(b, u):
                        if real(b - 1):
                            dispatch_move(b - 1, 1 - u)
                            low_combine(b - 1, 1 - u)
                        if real(b + 2):
                            stats(b + 2, u)
                        if real(b + 1):
                            normalize(b + 1, 1 - u)
                        if real(b):
                            dispatch_max(b, u)
                        if real(b + 1):
                            low_x(b + 1, 1 - u, range(1))
                        if real(b):
                            combine(b, u)
                        if real(b + 1):
                            low_x(b + 1, 1 - u, range(1, 2))
                        if real(b):
                            dispatch_scale(b, u)
                        if real(b + 1):
                            low_x(b + 1, 1 - u, range(2, 3))
                        if real(b):
                            combine_scale(b, u)
                        if real(b + 1):
                            low_x(b + 1, 1 - u, range(3, TPB))

                    stats(0, 0)
                    stats(1, 1)
                    normalize(0, 0)
                    slots_square()
                    low_x(0, 0, range(TPB))
                    slots_scale()
                    rounds(dve, round_)

                @block.scalar
                def _(act):
                    def move_x(b, u, tiles):
                        if later(b, 1):
                            act.wait_ge(s["lt"], b)
                        for t in tiles:
                            act.wait_ge(s["turned"], TPB * b + t + 1)
                            at = slice(t * P, (t + 1) * P)
                            k = (TPB * u + t) % 2
                            nc.scalar.activation(xh[:, :, at], ps_x[:, k, 0:2 * P].rearrange("p (k n) -> p k n", k=2),
                                                 ACT.Copy).then_inc(s["xh_ready"], 1)

                    def move_sums(b, u):
                        act.wait_ge(s["cturned"], b + 1)
                        nc.scalar.activation(ct_hi[:, b, :].rearrange("p (k n) -> p k n", k=2), ps_ct[0:NP_, :, 0:HT],
                                             ACT.Copy).then_inc(s["ct_hi_ready"], 1)
                        act.wait_ge(s["xtilde"], b + 1)
                        nc.scalar.activation(xr[:, b, :], ps_d[0:NP_, 256:256 + DIM], ACT.Copy).then_inc(s["xt_ready"], 1)

                    def exponentials(b, u):
                        act.wait_ge(s["lt"], b + 1)
                        if later(b, 1):
                            act.wait_ge(s["lc"], b)
                        nc.scalar.activation(logits[:, :].rearrange("p (k n) -> p k n", k=2), ps_l[0:NP_, :, 0:HT],
                                             ACT.Copy).then_inc(s["lt_moved"], 1)
                        if real(b + 1):
                            move_x(b + 1, 1 - u, range(1))
                        act.wait_ge(s["nmax"], b + 1)
                        if later(b, 2):
                            act.wait_ge(s["dturned"], b - 1)
                            act.wait_ge(s["rrec"], b - 1)
                        nc.scalar.activation(ed[:, u, :].rearrange("p (k n) -> p k n", k=2), ps_l[0:NP_, :, 0:HT], ACT.Exp,
                                             bias=top[:, u, :], accum_out=rs[:, u, :]).then_inc(s["exped"], 1)
                        if real(b + 1):
                            move_x(b + 1, 1 - u, range(1, 2))
                        act.wait_ge(s["cshift"], b + 1)
                        nc.scalar.activation(cl[:, u], cl[:, u], ACT.Exp).then_inc(s["cexp"], 1)

                    def round_(b, u):
                        if real(b - 1):
                            move_sums(b - 1, 1 - u)
                        if real(b):
                            exponentials(b, u)
                        if real(b + 1):
                            move_x(b + 1, 1 - u, range(2, TPB))

                    move_x(0, 0, range(TPB))
                    rounds(act, round_)

                @block.tensor
                def _(pe):
                    def turn_x(b, u, tiles):
                        pe.wait_ge(s["xnorm"], b + 1)
                        for t in tiles:
                            k = (TPB * u + t) % 2
                            if later(b, 1) or t >= 2:
                                pe.wait_ge(s["xl_ready"], TPB * b + t - 1)
                            nc.tensor.transpose(ps_x[:, k, 0:P], xn[:, u, t, 0:P], ident[:, :])
                            nc.tensor.transpose(ps_x[:, k, P:2 * P], xn[:, u, t, P:2 * P],
                                                ident[:, :]).then_inc(s["turned"], 1)

                    def sum_batch(b, u):
                        pe.wait_ge(s["escaled"], b + 1)
                        if later(b, 1):
                            pe.wait_ge(s["xt_ready"], b)
                            pe.wait_ge(s["ct_lo_ready"], b)
                        pe.wait_ge(s["cready"], b + 1)
                        for t in range(TPB):
                            c0 = t * P
                            for lo, hi in ((c0, min(c0 + P, HT)), (max(c0, HT), c0 + P)):
                                if lo < hi:
                                    k = lo // HT
                                    last = nc.tensor.transpose(ps_ct[0:NP_, k, lo - k * HT:hi - k * HT],
                                                               cl[lo - c0:hi - c0, u, t, :],
                                                               ident[lo - c0:hi - c0, lo - c0:hi - c0])
                        last.then_inc(s["cturned"], 1)
                        for t in range(TPB):
                            last = nc.tensor.transpose(ps_d[:, t * NP_:(t + 1) * NP_], ed[:, u, t * P:(t + 1) * P],
                                                       ident[0:NP_, 0:NP_])
                        last.then_inc(s["dturned"], 1)
                        pe.wait_ge(s["dt_ready"], b + 1)
                        for t in range(TPB):
                            last = nc.tensor.matmul(ps_d[0:NP_, 256:256 + DIM], dt_[:, u, t, :], xn[:, u, t, 0:DIM],
                                                    start=t == 0, stop=t == TPB - 1)
                        last.then_inc(s["xtilde"], 1)

                    def logits_of(b, u):
                        if later(b, 1):
                            pe.wait_ge(s["exped"], b)
                        else:
                            pe.wait_ge(s["sl_split"], 2)
                        pe.wait_ge(s["xl_ready"], TPB * (b + 1))
                        for k in range(2):
                            o = ps_l[0:NP_, k, 0:HT]
                            at = slice(k * HT, (k + 1) * HT)
                            nc.tensor.matmul(o, sl_hi[:, 0, :], xh[:, 0, at], start=True, stop=False)
                            nc.tensor.matmul(o, sl_lo[:, 0, :], xh[:, 0, at], start=False, stop=False)
                            nc.tensor.matmul(o, sl_hi[:, 0, :], xl[:, at], start=False, stop=False)
                            nc.tensor.matmul(o, sl_hi[:, 1, :], xh[:, 1, at], start=False, stop=False)
                            last = nc.tensor.matmul(o, sl_lo[0:TAIL, 1, :], xh[0:TAIL, 1, at], start=False, stop=True)
                        last.then_inc(s["lt"], 1)

                    def turn_logits(b, u):
                        if not real(b + 1):
                            pe.wait_ge(s["cshift"], b)
                            pe.wait_ge(s["lt_moved"], b + 1)
                        for t in range(TPB):
                            last = nc.tensor.transpose(ps_c[:, t * NP_:(t + 1) * NP_], logits[:, t * P:(t + 1) * P],
                                                       ident[0:NP_, 0:NP_])
                        last.then_inc(s["lc"], 1)

                    def round_(b, u):
                        if real(b - 1):
                            sum_batch(b - 1, 1 - u)
                        if real(b):
                            logits_of(b, u)
                            if real(b + 1):
                                if later(b, 1):
                                    pe.wait_ge(s["cshift"], b)
                                pe.wait_ge(s["lt_moved"], b + 1)
                                turn_x(b + 1, 1 - u, range(1))
                            turn_logits(b, u)
                            if real(b + 1):
                                turn_x(b + 1, 1 - u, range(1, TPB))

                    turn_x(0, 0, range(TPB))
                    rounds(pe, round_)

        with ExitStack() as two:
            ps_h = two.enter_context(nc.psum_tensor("ps_h4", [P, 512], F32))
            ps_y = two.enter_context(nc.psum_tensor("ps_y4", [P, 2, 512], F32))
            ps_r = two.enter_context(nc.psum_tensor("ps_r4", [P, 2, 512], F32))
            ps_o = two.enter_context(nc.psum_tensor("ps_o4", [P, 3, 512], F32))
            down, hid, up, biased, yturned, yr_hi_ready, yr_lo_ready, mixed, added, out_done = (
                sem(n) for n in ("down", "hid", "up", "biased", "yturned", "yr_hi_ready", "yr_lo_ready", "mixed", "added", "out_done"))
            BQ = BATCH * SLOTP
            GROUPS = [(0, 2), (2, 2), (4, 1)]

            with nc.Block() as block:
                @block.tensor
                def _(pe):
                    for b in range(BATCH):
                        for k, (c, rows) in enumerate(((0, P), (P, TAIL))):
                            last = nc.tensor.transpose(ps_r[0:rows, k, b * NP_:(b + 1) * NP_], xr[:, b, c:c + rows],
                                                       ident[0:NP_, 0:NP_])
                    last.then_inc(s["xtilde"], 1)
                    pe.wait_ge(s["xt_ready"], BATCH + 1)
                    for n in range(EXPERTS):
                        o = ps_h[0:HID, n * BQ:(n + 1) * BQ]
                        nc.tensor.matmul(o, wd[:, 0, n, :], xt[:, 0, n].rearrange("p b q -> p (b q)"), start=True, stop=False)
                        nc.tensor.matmul(o, wd[0:TAIL, 1, n, :], xt[0:TAIL, 1, n].rearrange("p b q -> p (b q)"),
                                         start=False, stop=True).then_inc(down, 1)
                    pe.wait_ge(hid, EXPERTS)
                    for n in range(EXPERTS):
                        for k, (c, rows) in enumerate(((0, P), (P, TAIL))):
                            last = nc.tensor.matmul(ps_y[0:rows, k, n * BQ:(n + 1) * BQ], wu[:, n, c:c + rows], ht[:, n, :],
                                                    start=True, stop=True)
                    last.then_inc(up, 1)
                    pe.wait_ge(biased, 2)
                    for b in range(BATCH):
                        if b >= 2:
                            pe.wait_ge(yr_lo_ready, b - 1)
                        for k, (c, rows) in enumerate(((0, P), (P, TAIL))):
                            last = nc.tensor.transpose(ps_r[0:NP_, b % 2, c:c + rows],
                                                       yt[0:rows, k, b].rearrange("p n q -> p (n q)"), ident[0:rows, 0:rows])
                        last.then_inc(yturned, 1)
                    for b in range(BATCH):
                        pe.wait_ge(yr_lo_ready, b + 1)
                        for g, (t0, nt) in enumerate(GROUPS):
                            if b >= 1:
                                pe.wait_ge(added, 3 * (b - 1) + g + 1)
                            for t in range(nt):
                                o = ps_o[:, g, t * DIM:(t + 1) * DIM]
                                at = slice((t0 + t) * P, (t0 + t + 1) * P)
                                nc.tensor.matmul(o, ct_hi[:, b, at], yr_hi[:, b, :], start=True, stop=False)
                                nc.tensor.matmul(o, ct_hi[:, b, at], yr_lo[:, b, :], start=False, stop=False)
                                last = nc.tensor.matmul(o, ct_lo[:, b, at], yr_hi[:, b, :], start=False, stop=True)
                            last.then_inc(mixed, 1)

                @block.scalar
                def _(act):
                    act.wait_ge(s["xtilde"], BATCH + 1)
                    for k, rows in enumerate((P, TAIL)):
                        last = nc.scalar.activation(
                            xt[0:rows, k], ps_r[0:rows, k, 0:BATCH * NP_].rearrange("p (b n q) -> p n b q", b=BATCH, n=EXPERTS),
                            ACT.Copy)
                    last.then_inc(s["xt_ready"], 1)
                    for n in range(EXPERTS):
                        act.wait_ge(down, EXPERTS)
                        nc.scalar.activation(ht[:, n, :], ps_h[0:HID, n * BQ:(n + 1) * BQ], ACT.Gelu,
                                             bias=bd[:, n:n + 1]).then_inc(hid, 1)
                    for b in range(BATCH):
                        act.wait_ge(yturned, b + 1)
                        nc.scalar.activation(yr_hi[:, b, :], ps_r[0:NP_, b % 2, 0:DIM], ACT.Copy).then_inc(yr_hi_ready, 1)

                @block.vector
                def _(dve):
                    dve.wait_ge(up, 1)
                    for k, rows in enumerate((P, TAIL)):
                        nc.vector.tensor_tensor(
                            yt[0:rows, k].rearrange("p b n q -> p n b q"),
                            ps_y[0:rows, k, 0:EXPERTS * BQ].rearrange("p (n b q) -> p n b q", n=EXPERTS, b=BATCH),
                            bu[0:rows, k, :].unsqueeze(2).unsqueeze(3).broadcast_to([rows, EXPERTS, BATCH, SLOTP]),
                            ALU.add).then_inc(biased, 1)
                    for b in range(BATCH):
                        dve.wait_ge(yr_hi_ready, b + 1)
                        nc.vector.tensor_tensor(yr_lo[:, b, :], ps_r[0:NP_, b % 2, 0:DIM], yr_hi[:, b, :],
                                                ALU.subtract).then_inc(yr_lo_ready, 1)
                    for b in range(BATCH):
                        for g, (t0, nt) in enumerate(GROUPS):
                            dve.wait_ge(mixed, 3 * b + g + 1)
                            rows = h[:, TPB * b + t0:TPB * b + t0 + nt, :]
                            nc.vector.tensor_tensor(rows, ps_o[:, g, 0:nt * DIM].rearrange("p (t d) -> p t d", t=nt), rows,
                                                    ALU.add).then_inc(added, 1)

                @block.sync
                def _(sp):
                    for b in range(BATCH):
                        sp.wait_ge(added, 3 * (b + 1))
                        sp.dma_start(out[b].rearrange("(t p) d -> p t d", p=P),
                                     h[:, TPB * b:TPB * (b + 1), :]).then_inc(out_done, 16)
                    sp.wait_ge(out_done, 16 * BATCH)


def early_fusion_kernel(nc, a, out):
    with ExitStack() as ctx:
        def sb(name, shape, dt):
            return ctx.enter_context(nc.sbuf_tensor(name, shape, dt))

        h = sb("h", [P, TILES, DIM], F32)
        ident = sb("ident", [P, P], F32)
        staging = sb("staging", [P, QCOLS // P * INNER // 2], F32)
        NQ = G * HEADS // 2 * 2 * P
        wq_t = staging[:, 0:NQ].rearrange("p (n c) -> p n c", c=2 * P)
        kv_f = staging[:, NQ:NQ + 4 * INNER].rearrange("p (k c) -> p k c", k=2)
        tokenizer(nc, a['x'], a['txt'], a['bands'], a['tok_w'], h, ident, staging,
                  [(wq_t, a['wq_t']), (kv_f, a['kv_w'])])
        with ExitStack() as attn:
            def sa(name, shape, dt):
                return attn.enter_context(nc.sbuf_tensor(name, shape, dt))

            stats = sa("stats", [P, TILES, 2], F32)
            kv_hi = sa("kvs_hi", [P, BATCH, HEADS, KVW], BF16)
            kv_lo = sa("kvs_lo", [P, BATCH, HEADS, KVW], BF16)
            w = {'gt': sa("gt", [P, G], F32), 'betat': sa("betat", [P, G], F32), 'gf': sa("gf", [P, INNER // P], F32),
                 'betaf': sa("betaf", [P, INNER // P], F32), 'bf': sa("bf", [P, INNER], F32),
                 'eps': sa("eps", [P, 8], F32), 'bo': sa("bo", [P, DIM], F32), 'half': sa("half", [P, TILES], F32),
                 'q_hi': sa("q_hi", [P, 2, QCOLS], BF16), 'q_lo': sa("q_lo", [P, 2, QCOLS], BF16),
                 'wo_hi': sa("wo_hi", [P, INNER // P, DIM], BF16), 'wo_lo': sa("wo_lo", [P, INNER // P, DIM], BF16)}
            shared = sa("shared", [P, 2, 2 * INNER], F32)
            w['kv_hi'], w['kv_lo'] = (shared[:, n].bitcast(BF16).rearrange("p (k c) -> p k c", k=2) for n in range(2))
            attention_weights(nc, a, w, wq_t, kv_f, stats, h, ident)
            w['wf_hi'] = staging[:, :].bitcast(BF16).rearrange("p (c n) -> p c n", n=INNER)
            w['wf_lo'] = sa("wf_lo", [P, QCOLS // P, INNER], BF16)
            keys_and_values(nc, a, w, kv_hi, kv_lo, stats, h, ident)
            attend(nc, w, shared, kv_hi, kv_lo, stats, h, ident)
        soft_experts(nc, a, out, h, ident)


_OUTS = [((8, 640, 192), 'float32')]


def _layout(i):
    import numpy as _np

    f = {k: _np.asarray(v) for k, v in i.items()}
    q = COORDS - TAIL
    x = f['x'].reshape(BATCH, 2, HALF, COORDS).transpose(0, 1, 3, 2)
    x = _np.concatenate([x, x[:, :, q:]], axis=2).reshape(BATCH, 2, FULL + 1, P, HALF).transpose(0, 1, 3, 2, 4)
    t = f['L0_tok_W'].reshape(DIM, COORDS, 2, BANDS).transpose(2, 1, 3, 0)
    sines, cosines = (t[k, 0:q].reshape(FULL, P, BANDS, DIM).transpose(1, 2, 0, 3) for k in range(2))
    tail = t[:, q:].reshape(P, BANDS, 1, DIM)
    tok_w = _np.concatenate([sines, tail, cosines], axis=2)

    def tails(v):
        return _np.stack([v[0:P], _np.concatenate([v[P:], v[P:]])], axis=1)

    kv_w = tails(_np.concatenate([f['L0_attn_Wk'], f['L0_attn_Wv']], axis=1))
    wq = f['L0_attn_Wq'].reshape(G, DIM, HEADS // 2, P).transpose(3, 0, 2, 1).reshape(P, G * HEADS // 2, DIM)
    wq_t = _np.concatenate([wq, wq[:, :, P:]], axis=2)
    wt_diag = _np.zeros((P, G, P), f['L0_attn_Wt'].dtype)
    bias_rows = _np.zeros((P - TAIL, G, HEADS, DH), f['L0_attn_bt'].dtype)
    for k in range(2):
        wt_diag[k * DH:(k + 1) * DH, :, k * DH:(k + 1) * DH] = f['L0_attn_Wt'].transpose(1, 0, 2)
        bias_rows[32 * k] = f['L0_attn_bt'][:, None, :]

    def twice(v):
        return _np.concatenate([v.T, v.T])

    def columns(v):
        return v.reshape(-1, P).T

    return {
        'x': x, 'txt': f['txt'], 'bands': f['L0_tok_freq_bands'], 'tok_w': tok_w, 'kv_w': kv_w, 'wq_t': wq_t,
        'wt_diag': wt_diag, 'bias_rows': bias_rows.reshape(P - TAIL, QCOLS),
        'gt': twice(f['L0_attn_gt']), 'betat': twice(f['L0_attn_betat']),
        'wf': f['L0_attn_Wf'].reshape(QCOLS // P, P, INNER), 'bf': f['L0_attn_bf'],
        'gf': columns(f['L0_attn_gf']), 'betaf': columns(f['L0_attn_betaf']),
        'slots': tails(f['L0_ffn_slot_params'].reshape(DIM, NP_)), 'scale': f['L0_ffn_scale'].reshape(1),
        'w_down': tails(f['L0_ffn_W_down'].transpose(1, 0, 2)), 'b_down': f['L0_ffn_b_down'].T,
        'w_up': f['L0_ffn_W_up'].transpose(1, 0, 2), 'b_up': tails(f['L0_ffn_b_up'].T),
        'wo': f['L0_attn_Wo'].reshape(INNER // P, P, DIM).transpose(1, 0, 2), 'bo': f['L0_attn_bo'],
    }


def kernel(**inputs):
    import numpy as _np
    import concourse.bacc as _bacc
    from concourse import mybir as _mybir
    from concourse.bass_utils import run_bass_kernel_spmd as _run

    nc = _bacc.Bacc("TRN2", target_bir_lowering=False, num_devices=1)
    arrays, args = {}, {}
    for name, a in _layout(inputs).items():
        arrays[f"in_{name}_dram"] = _np.ascontiguousarray(a)
        args[name] = nc.dram_tensor(f"in_{name}_dram", a.shape, _mybir.dt.from_np(a.dtype), kind="ExternalInput").ap()
    shape, dtype = _OUTS[0]
    out = nc.dram_tensor("out_0_dram", shape, _mybir.dt.from_np(_np.dtype(dtype)), kind="ExternalOutput").ap()
    early_fusion_kernel(nc, args, out)
    r = _run(nc, [arrays], core_ids=[0])
    return r.results[0]["out_0_dram"]
```
